# Optimizing a Trainium2 kernel written in Bass

```python
import numpy as np
import jax
import jax.numpy as jnp

def _softmax(x, axis=-1):
    return jax.nn.softmax(x, axis=axis)

def _gelu(x):
    return jax.nn.gelu(x, approximate=True)

def _silu(x):
    return jax.nn.silu(x)

def _sigmoid(x):
    return jax.nn.sigmoid(x)

def _layernorm(x, axis=-1, eps=1e-05):
    m = jnp.mean(x, axis=axis, keepdims=True)
    v = jnp.var(x, axis=axis, keepdims=True)
    return (x - m) / jnp.sqrt(v + eps)

def _scatter_add(tgt, idx, src, axis=0):
    return tgt.at[idx].add(src)

def _segment_sum(src, seg, n):
    return jax.ops.segment_sum(src, seg, n)
kernel_name = 'mk_flamingo_gated_d1_seqx_r8_f89165'

def setup_inputs(seed: int=0):
    np.random.seed(seed)
    _w = jnp.asarray

    def _rec_inputs():
        import jax
        import jax.numpy as jnp
        _rk = jax.random.key(seed)
        x = 7.22e-05 + 1 * jax.random.normal(jax.random.fold_in(_rk, 1), (4, 256, 128), jnp.float32)
        _lenS = 256 - jax.random.randint(jax.random.fold_in(_rk, 7), (4,), 0, max(1, 256 // 4) + 1, jnp.int32)
        _lenS2 = 512 - jax.random.randint(jax.random.fold_in(_rk, 8), (4,), 0, max(1, 512 // 4) + 1, jnp.int32)
        _ctx_1024P = jax.random.normal(jax.random.fold_in(_rk, 11), (4, 16, 128), jnp.float32)
        _ctx_1024c = jax.random.dirichlet(jax.random.fold_in(_rk, 511), 0.3 * jnp.ones((16,), jnp.float32), (4, 512))
        _ctx_1024t = jnp.einsum('bsk,bkd->bsd', _ctx_1024c, _ctx_1024P)
        _ctx_1024t = _ctx_1024t * jax.lax.rsqrt(jnp.mean(jnp.square(_ctx_1024t)) + 1e-12) * 0.953939
        ctx_1024 = -1.39393e-06 + 0.999914 * (_ctx_1024t + 0.3 * jax.random.normal(jax.random.fold_in(_rk, 611), (4, 512, 128), jnp.float32))
        _g = jax.random.normal(jax.random.fold_in(_rk, 9001), (2, 1), jnp.float32)
        _g = jnp.sign(_g) * jnp.maximum(jnp.abs(_g), 1.0) + (_g == 0) * 1.0
        g_xattn = _g[0]
        g_ffn = _g[1]
        return (x, ctx_1024, g_xattn, g_ffn)
    x, ctx_1024, g_xattn, g_ffn = _rec_inputs()

    def _L0_xattn_setup():
        import jax, jax.numpy as jnp
        import numpy as np
        DIM = 128
        CTX_DIM = 128
        HEADS = 16
        DIM_HEAD = 64
        INNER = HEADS * DIM_HEAD
        FF_INNER = 4 * DIM
        EPS = 1e-05

        def layer_norm(x, g, b):
            mu = jnp.mean(x, axis=-1, keepdims=True)
            var = jnp.var(x, axis=-1, keepdims=True)
            return (x - mu) * jax.lax.rsqrt(var + EPS) * g + b
        key = jax.random.key(seed)
        ks = jax.random.split(key, 9)
        b, n, j = (4, 256, 128)
        inp = {'x': jax.random.normal(ks[0], (b, n, DIM), dtype=jnp.float32), 'context': jax.random.normal(ks[1], (b, j, CTX_DIM), dtype=jnp.float32), 'ln_g': jnp.ones((DIM,), jnp.float32), 'ln_b': jnp.zeros((DIM,), jnp.float32), 'cln_g': jnp.ones((CTX_DIM,), jnp.float32), 'cln_b': jnp.zeros((CTX_DIM,), jnp.float32), 'Wq': jax.random.normal(ks[2], (DIM, INNER), dtype=jnp.float32) * DIM ** (-0.5), 'Wkv': jax.random.normal(ks[3], (CTX_DIM, 2 * DIM_HEAD), dtype=jnp.float32) * CTX_DIM ** (-0.5), 'Wo': jax.random.normal(ks[4], (INNER, DIM), dtype=jnp.float32) * INNER ** (-0.5), 'Wff1': jax.random.normal(ks[5], (DIM, 2 * FF_INNER), dtype=jnp.float32) * DIM ** (-0.5), 'Wff2': jax.random.normal(ks[6], (FF_INNER, DIM), dtype=jnp.float32) * FF_INNER ** (-0.5)}
        return inp
    _L0_xattn_all = _L0_xattn_setup()
    _L0_xattn_in = {k: v for k, v in _L0_xattn_all.items() if k in ('ln_g', 'ln_b', 'cln_g', 'cln_b', 'Wq', 'Wkv', 'Wo', 'Wff1', 'Wff2')}
    del _L0_xattn_all

    def _L0_ffn_setup():
        import jax, jax.numpy as jnp
        import numpy as np
        E, H, I = (8, 128, 64)
        NG, TKG, TOPK = (4, 2, 4)
        SCALE = 2.5

        def _mlp(x, wg, wu, wd):
            return jax.nn.silu(x @ wg) * (x @ wu) @ wd
        key = jax.random.key(seed)
        ks = jax.random.split(key, 8)
        s = 0.02
        return {'hidden_states': jax.random.normal(ks[0], (32, 32, H), jnp.float32), 'gate_w': jax.random.normal(ks[1], (E, H), jnp.float32) * np.float32(np.sqrt(2.0 / H)), 'correction_bias': jnp.zeros((E,), jnp.float32), 'Wg': jax.random.normal(ks[2], (E, H, I), jnp.float32) * s, 'Wu': jax.random.normal(ks[3], (E, H, I), jnp.float32) * s, 'Wd': jax.random.normal(ks[4], (E, I, H), jnp.float32) * s, 'Wg_s': jax.random.normal(ks[5], (H, I), jnp.float32) * s, 'Wu_s': jax.random.normal(ks[6], (H, I), jnp.float32) * s, 'Wd_s': jax.random.normal(ks[7], (I, H), jnp.float32) * s}
    _L0_ffn_all = _L0_ffn_setup()
    _L0_ffn_in = {k: v for k, v in _L0_ffn_all.items() if k in ('gate_w', 'correction_bias', 'Wg', 'Wu', 'Wd', 'Wg_s', 'Wu_s', 'Wd_s')}
    del _L0_ffn_all
    return {'x': x, 'ctx_1024': ctx_1024, 'g_xattn': g_xattn, 'g_ffn': g_ffn, 'L0_xattn_ln_g': _L0_xattn_in['ln_g'], 'L0_xattn_ln_b': _L0_xattn_in['ln_b'], 'L0_xattn_cln_g': _L0_xattn_in['cln_g'], 'L0_xattn_cln_b': _L0_xattn_in['cln_b'], 'L0_xattn_Wq': _L0_xattn_in['Wq'], 'L0_xattn_Wkv': _L0_xattn_in['Wkv'], 'L0_xattn_Wo': _L0_xattn_in['Wo'], 'L0_xattn_Wff1': _L0_xattn_in['Wff1'], 'L0_xattn_Wff2': _L0_xattn_in['Wff2'], 'L0_ffn_gate_w': _L0_ffn_in['gate_w'], 'L0_ffn_correction_bias': _L0_ffn_in['correction_bias'], 'L0_ffn_Wg': _L0_ffn_in['Wg'], 'L0_ffn_Wu': _L0_ffn_in['Wu'], 'L0_ffn_Wd': _L0_ffn_in['Wd'], 'L0_ffn_Wg_s': _L0_ffn_in['Wg_s'], 'L0_ffn_Wu_s': _L0_ffn_in['Wu_s'], 'L0_ffn_Wd_s': _L0_ffn_in['Wd_s']}

def reference(x, ctx_1024, g_xattn, g_ffn, L0_xattn_ln_g, L0_xattn_ln_b, L0_xattn_cln_g, L0_xattn_cln_b, L0_xattn_Wq, L0_xattn_Wkv, L0_xattn_Wo, L0_xattn_Wff1, L0_xattn_Wff2, L0_ffn_gate_w, L0_ffn_correction_bias, L0_ffn_Wg, L0_ffn_Wu, L0_ffn_Wd, L0_ffn_Wg_s, L0_ffn_Wu_s, L0_ffn_Wd_s):
    import jax
    import jax.numpy as jnp

    def _L0_xattn_ref(x, context, ln_g, ln_b, cln_g, cln_b, Wq, Wkv, Wo, Wff1, Wff2):
        import jax, jax.numpy as jnp
        import numpy as np
        DIM = 128
        CTX_DIM = 128
        HEADS = 16
        DIM_HEAD = 64
        INNER = HEADS * DIM_HEAD
        FF_INNER = 4 * DIM
        EPS = 1e-05

        def layer_norm(x, g, b):
            mu = jnp.mean(x, axis=-1, keepdims=True)
            var = jnp.var(x, axis=-1, keepdims=True)
            return (x - mu) * jax.lax.rsqrt(var + EPS) * g + b
        scale = DIM_HEAD ** (-0.5)
        xn = layer_norm(x, ln_g, ln_b)
        cn = layer_norm(context, cln_g, cln_b)
        b, n, _ = xn.shape
        q = (xn @ Wq).reshape(b, n, HEADS, DIM_HEAD).transpose(0, 2, 1, 3) * scale
        kv = cn @ Wkv
        k, v = (kv[..., :DIM_HEAD], kv[..., DIM_HEAD:])
        sim = jnp.einsum('bhid,bjd->bhij', q, k)
        attn = jax.nn.softmax(sim, axis=-1)
        out = jnp.einsum('bhij,bjd->bhid', attn, v)
        out = out.transpose(0, 2, 1, 3).reshape(b, n, INNER) @ Wo
        ff = xn @ Wff1
        h, gate = (ff[..., :FF_INNER], ff[..., FF_INNER:])
        out = out + jax.nn.silu(gate) * h @ Wff2
        return out

    def _L0_ffn_ref(hidden_states, gate_w, correction_bias, Wg, Wu, Wd, Wg_s, Wu_s, Wd_s):
        import jax, jax.numpy as jnp
        import numpy as np
        E, H, I = (8, 128, 64)
        NG, TKG, TOPK = (4, 2, 4)
        SCALE = 2.5

        def _mlp(x, wg, wu, wd):
            return jax.nn.silu(x @ wg) * (x @ wu) @ wd
        B, T, _ = hidden_states.shape
        x = hidden_states.reshape(-1, H)
        N = x.shape[0]
        logits = x @ gate_w.T
        scores = jax.nn.sigmoid(logits)
        scores_c = scores + correction_bias
        grp = scores_c.reshape(N, NG, E // NG)
        group_scores = jnp.sum(jax.lax.top_k(grp, 2)[0], axis=-1)
        grp_idx = jax.lax.top_k(group_scores, TKG)[1]
        group_mask = jnp.zeros_like(group_scores).at[jnp.arange(N)[:, None], grp_idx].set(1.0)
        score_mask = jnp.repeat(group_mask, E // NG, axis=-1) > 0.5
        scores_for_choice = jnp.where(score_mask, scores_c, 0.0)
        topk_idx = jax.lax.top_k(scores_for_choice, TOPK)[1]
        topk_w = jnp.take_along_axis(scores, topk_idx, axis=-1)
        topk_w = topk_w / (jnp.sum(topk_w, axis=-1, keepdims=True) + 1e-20)
        topk_w = topk_w * SCALE
        cw = jnp.sum(jax.nn.one_hot(topk_idx, E, dtype=topk_w.dtype) * topk_w[..., None], axis=1)
        g = jnp.einsum('nh,ehi->eni', x, Wg)
        u = jnp.einsum('nh,ehi->eni', x, Wu)
        y = jnp.einsum('eni,eih->enh', jax.nn.silu(g) * u, Wd)
        routed = jnp.einsum('enh,ne->nh', y, cw)
        out = routed + _mlp(x, Wg_s, Wu_s, Wd_s)
        return out.reshape(B, T, H)
    x = x + jnp.tanh(g_xattn[0]) * _L0_xattn_ref(_layernorm(x, axis=-1), ctx_1024, L0_xattn_ln_g, L0_xattn_ln_b, L0_xattn_cln_g, L0_xattn_cln_b, L0_xattn_Wq, L0_xattn_Wkv, L0_xattn_Wo, L0_xattn_Wff1, L0_xattn_Wff2)
    x = x + jnp.tanh(g_ffn[0]) * _L0_ffn_ref(_layernorm(x, axis=-1), L0_ffn_gate_w, L0_ffn_correction_bias, L0_ffn_Wg, L0_ffn_Wu, L0_ffn_Wd, L0_ffn_Wg_s, L0_ffn_Wu_s, L0_ffn_Wd_s)
    return x

_drawn_inputs = setup_inputs


def setup_inputs(seed=0):
    import zlib

    import numpy as np

    out = dict(_drawn_inputs(seed))
    spreads = {'L0_xattn_ln_g': (1.0, 0.2),
     'L0_xattn_ln_b': (0.0, 0.1),
     'L0_xattn_cln_g': (1.0, 0.2),
     'L0_xattn_cln_b': (0.0, 0.1),
     'L0_ffn_correction_bias': (0.0, 0.8)}
    factors = {'L0_ffn_gate_w': 8.0,
     'L0_ffn_Wg': 8.0,
     'L0_ffn_Wu': 8.0,
     'L0_ffn_Wd': 8.0,
     'L0_ffn_Wg_s': 8.0,
     'L0_ffn_Wu_s': 8.0,
     'L0_ffn_Wd_s': 8.0}
    for name, (base, spread) in spreads.items():
        noise = np.random.default_rng([zlib.crc32(name.encode()), seed]).standard_normal(out[name].shape)
        drawn = base * np.exp(spread * noise) if base else spread * noise
        out[name] = jnp.asarray(drawn.astype(out[name].dtype))
    for name, factor in factors.items():
        out[name] = (out[name] * factor).astype(out[name].dtype)
    return out
```

```python
from contextlib import ExitStack

import concourse.bass as bass
from concourse import mybir

P = 128
F32 = mybir.dt.float32
F16 = mybir.dt.float16
ALU = mybir.AluOpType
ACT = mybir.ActivationFunctionType
AX_X = mybir.AxisListType.X


def flamingo_gated_moe(nc, x, ctx_in, g_xattn, g_ffn, ln_g, ln_b, cln_g, cln_b, Wq, Wkv, Wo, Wff1, Wff2,
                       gate_wT, cbias, Wg, Wu, Wd, Wg_s, Wu_s, Wd_s, out):
    B, N, DIM = x.shape
    J = ctx_in.shape[1]
    INNER = Wq.shape[1]
    DH = Wkv.shape[1] // 2
    H = INNER // DH
    FF = Wff2.shape[0]
    E, _, I = Wg.shape
    NG, TKG, TOPK, ROUTE_SCALE = 4, 2, 4, 2.5
    EPG = E // NG
    assert DIM == P and 2 * DH == P and 2 * I == P and J % P == 0 and N % P == 0
    EPS = 1e-5
    SM_SCALE = DH ** -0.5
    SHIFT = 16.0
    TOK = B * N
    XT = TOK // P
    CT = B * J // P
    IT = N // P
    JT = J // P
    HP = H // 2
    FT = FF // P
    EP = E // 2
    CH = 512
    NCH = TOK // CH
    TPC = CH // P
    VW = 2 * DH + 1
    UNITS = B * HP
    CHUNKS = 2 * UNITS

    with ExitStack() as stack:
        def sb(name, shape, dt=F32):
            return stack.enter_context(nc.sbuf_tensor(name, shape, dt))

        def sem(name):
            return stack.enter_context(nc.semaphore(name))

        psM = stack.enter_context(nc.psum_tensor("psM", [P, 2, 512], F32))
        psS = stack.enter_context(nc.psum_tensor("psS", [P, 4, 512], F32))
        psO = stack.enter_context(nc.psum_tensor("psO", [P, 2, 512], F32))

        xs = sb("xs", [P, XT, DIM])
        yx = sb("yx", [P, XT, DIM])
        cs = sb("cs", [P, CT, DIM])
        stats = sb("stats", [P, XT + CT, 6])
        mv = sb("mv", [P, XT + CT, 2])
        rstd = sb("rstd", [P, XT + CT])
        rstd2 = sb("rstd2", [P, XT + CT])
        xnT = sb("xnT", [P, TOK])
        cnT = sb("cnT", [P, B * J])
        wq = sb("wq", [P, INNER])
        wkk = sb("wkk", [P, 2 * DH])
        wv = sb("wv", [P, DH])
        wo = sb("wo", [P, HP, DIM])
        wf1 = sb("wf1", [P, 2 * FF])
        wf2 = sb("wf2", [P, FT, DIM])
        wg = sb("wg", [P, E, I])
        wu = sb("wu", [P, E, I])
        wd = sb("wd", [P, EP, DIM])
        wgs = sb("wgs", [P, I])
        wus = sb("wus", [P, I])
        wds = sb("wds", [I, DIM])
        gw = sb("gw", [P, E])
        cb = sb("cb", [P, E])
        lnp = sb("lnp", [P, 4])
        gates = sb("gates", [P, 2])
        tg = sb("tg", [P, 2])
        ident = sb("ident", [P, P])
        ident16 = sb("ident16", [P, P], F16)
        lower = sb("lower", [P, E, E])
        esel = sb("esel", [E, EP, 2, I])
        qa = sb("qa", [P, H, TOK], F16)
        qb = sb("qb", [DH + 1, 2, H, N], F16)
        ka = sb("ka", [P, B * J], F16)
        kb = sb("kb", [DH + 1, B * J], F16)
        vm = sb("vm", [P, CT, VW], F16)
        mx = sb("mx", [P, B, IT, H])
        c16 = sb("c16", [P, B, IT, H], F16)
        cT = sb("cT", [H, B, N], F16)
        p32 = sb("p32", [P, 4, 2 * CH])
        ph = sb("ph", [P, 4, 2 * CH], F16)
        pl = sb("pl", [P, 4, 2 * CH], F16)
        olow = sb("olow", [P, 2, 2, IT, DH])
        osum = sb("osum", [P, 2, 2, IT, DH])
        rden = sb("rden", [P, 2, 2, IT])
        on = sb("on", [P, 2, IT, H, DH])
        oT = sb("oT", [P, HP, 2, N])
        sg = sb("sg", [P, 2, CH])
        ffT = sb("ffT", [P, FT, TOK])
        x1 = xs
        y2T = xnT
        hE = qa[:, :, :].rearrange("p h t -> p (h t)").bitcast(F32)[:, 0:(EP + 1) * TOK].rearrange("p (e t) -> p e t", t=TOK)
        es = sb("es", [P, TPC, E])
        sc = sb("sc", [P, TPC, E])
        scc = sb("scc", [P, TPC, E])
        grp = sb("grp", [P, TPC, NG])
        cmpA = p32[:, 0, 0:TPC * E * E].rearrange("p (t e f) -> p t e f", e=E, f=E)
        cmpB = p32[:, 1, 0:TPC * E * E].rearrange("p (t e f) -> p t e f", e=E, f=E)
        gsel = sb("gsel", [P, TPC, NG])
        choice = sb("choice", [P, TPC, E])
        rank = sb("rank", [P, TPC, E])
        grank = sb("grank", [P, TPC, NG])
        wsum = sb("wsum", [P, TPC])
        cw = sb("cw", [P, TPC, E])
        cwT = p32[0:E, 2, :].rearrange("e (c t) -> e c t", c=NCH)
        outt = cs

        ld_x = [sem(f"ld_x{b}") for b in range(B)]
        ld_c = [sem(f"ld_c{b}") for b in range(B)]
        ld_p = sem("ld_p")
        ld_k, ld_q = sem("ld_k"), sem("ld_q")
        ld_f, ld_o, ld_m = sem("ld_f"), sem("ld_o"), sem("ld_m")
        consts = sem("consts")
        chain = sem("chain")
        tg_ready = sem("tg_ready")
        var_ready = sem("var_ready")
        std_ready = sem("std_ready")
        z_ready = sem("z_ready")
        m_ready = [sem(f"m_ready{i}") for i in range(2)]
        xnT_ready, cnT_ready = sem("xnT_ready"), sem("cnT_ready")
        ka_ready, kb_ready = sem("ka_ready"), sem("kb_ready")
        vh_ready, vl_ready = sem("vh_ready"), sem("vl_ready")
        qh_ready, ql_ready = sem("qh_ready"), sem("ql_ready")
        qb_ready = sem("qb_ready")
        mx_ready = sem("mx_ready")
        c16_ready, cT_ready, crow_ready = sem("c16_ready"), sem("cT_ready"), sem("crow_ready")
        s_ready = sem("s_ready")
        ph_ready = sem("ph_ready")
        p32_ready = sem("p32_ready")
        pl_dve, pl_pool = sem("pl_dve"), sem("pl_pool")
        o_ready, ol_ready, os_ready, on_ready = sem("o_ready"), sem("ol_ready"), sem("os_ready"), sem("on_ready")
        rden_ready = sem("rden_ready")
        oT_ready = sem("oT_ready")
        sg_ready, ff_ready = sem("sg_ready"), sem("ff_ready")
        x1_ready = sem("x1_ready")
        var2_ready, std2_ready = sem("var2_ready"), sem("std2_ready")
        y2_ready, y2T_ready = sem("y2_ready"), sem("y2T_ready")
        t_ready = [sem(f"t_ready{i}") for i in range(8)]
        es_ready, cw_ready, cwT_ready = sem("es_ready"), sem("cw_ready"), sem("cwT_ready")
        hE_ready = sem("hE_ready")
        out_ready, stored = sem("out_ready"), sem("stored")

        tasks, order = [], []

        def task(*t):
            order.append(("task", len(tasks)))
            tasks.append(t)

        def project(b):
            return [("XT", b), ("CT", b), ("K", b)] + [("Q", b, p) for p in range(HP)] + [("V", b)]

        def maxima(b):
            return [("M", b, h, it) for h in range(H) for it in range(IT)] + [("C", b)]

        for t in project(0):
            task(*t)
        ffs = [("F", ft, c, half) for c in range(NCH) for ft in range(FT) for half in range(2)]
        for b in range(1, B):
            task("XT", b)
            task("CT", b)
        mm = maxima(0)
        while mm or ffs:
            for t in mm[:3]:
                task(*t)
            mm = mm[3:]
            for t in ffs[:2]:
                task(*t)
            ffs = ffs[2:]
        for b in range(B):
            side = []
            if b >= 1:
                for it in range(IT):
                    side += [("T", b - 1, it, 0), ("T", b - 1, it, 1), ("W", IT * (b - 1) + it)]
            if b + 1 < B:
                side += project(b + 1)[2:] + maxima(b + 1)
            per = -(-len(side) // HP) if side else 0
            for hp in range(HP):
                u = b * HP + hp
                order.append(("S", u, 0))
                now, side = side[:per], side[per:]
                first = per // 2 if hp else 0
                for t in now[:first]:
                    task(*t)
                order.append(("S", u, 1))
                if u >= 1:
                    order.append(("PV", u - 1))
                for t in now[first:]:
                    task(*t)
        order.append(("PV", UNITS - 1))
        for it in range(IT):
            task("T", B - 1, it, 0)
            task("T", B - 1, it, 1)
            task("W", IT * (B - 1) + it)

        tail = []
        for c in range(NCH):
            tail += [("YT", c), ("L", c)]
        for c in range(NCH):
            for p in range(EP + 1):
                tail += [("EG", c, p), ("EU", c, p)]
                if p == 1:
                    tail += [("CWT", c)]
            tail += [("CB", c, p) for p in range(EP)]
            tail += [("D", c * TPC + t) for t in range(TPC)]

        def count(kind, items, upto):
            return sum(1 for t in items[:upto] if t[0] == kind)

        pool_halves = [n for n in range(CHUNKS) if n % 5 in (0, 2, 4)]
        pooled = set(pool_halves)

        def wait_split(eng, n):
            if n in pooled:
                eng.wait_ge(pl_pool, sum(1 for m in pooled if m <= n))
            else:
                eng.wait_ge(pl_dve, n + 1 - sum(1 for m in pooled if m <= n))

        def mbank(n):
            return psM[:, n % 2, :]

        banks = [psM[:, 0, :], psM[:, 1, :]] + [psS[:, i, :] for i in range(4)] + [psO[:, i, :] for i in range(2)]

        def m_read(n):
            t = tasks[n]
            same = count(t[0], tasks, n) + 1
            if t[0] == "F":
                return (sg_ready, (same + 1) // 2) if t[3] == 0 else (ff_ready, same // 2)
            return {"XT": xnT_ready, "CT": cnT_ready, "K": kb_ready, "V": vl_ready, "Q": ql_ready, "M": mx_ready,
                    "C": cT_ready, "T": oT_ready, "W": x1_ready}[t[0]], same

        hE_at = {t: i + 1 for i, t in enumerate(t for t in tail if t[0] in ("EU", "CB"))}

        def t_read(n):
            t = tail[n]
            if t in hE_at:
                return hE_ready, hE_at[t]
            same = count(t[0], tail, n) + 1
            if t[0] == "EG":
                return sg_ready, FT * NCH + same
            return {"YT": y2T_ready, "L": es_ready, "CWT": cwT_ready, "D": out_ready}[t[0]], same

        block = stack.enter_context(nc.Block())

        @block.sync
        def _(sp):
            x_t = x.rearrange("b (t p) d -> p (b t) d", p=P)
            c_t = ctx_in.rearrange("b (t p) d -> p (b t) d", p=P)
            for b in range(B):
                sp.dma_start(xs[:, IT * b:IT * (b + 1), :], x_t[:, IT * b:IT * (b + 1), :]).then_inc(ld_x[b], 16)
                sp.dma_start(cs[:, JT * b:JT * (b + 1), :], c_t[:, JT * b:JT * (b + 1), :]).then_inc(ld_c[b], 16)
                if b == 0:
                    sp.dma_start(wkk[:, 0:DH], Wkv[:, 0:DH]).then_inc(ld_k, 16)
                    sp.dma_start(wkk[:, DH:2 * DH], Wkv[:, 0:DH]).then_inc(ld_k, 16)
                    sp.dma_start(wv[:, :], Wkv[:, DH:2 * DH]).then_inc(ld_k, 16)
                    sp.dma_start(wq[:, :], Wq).then_inc(ld_q, 16)
            sp.dma_start(wf1[:, :], Wff1).then_inc(ld_f, 16)
            sp.dma_start(wo[:, :, :], Wo.rearrange("(p r) d -> r p d", r=P)).then_inc(ld_o, 16)
            sp.dma_start(wf2[:, :, :], Wff2.rearrange("(p r) d -> r p d", r=P)).then_inc(ld_o, 16)
            sp.dma_start(wg[:, :, :], Wg.rearrange("e h i -> h e i")).then_inc(ld_m, 16)
            sp.dma_start(wu[:, :, :], Wu.rearrange("e h i -> h e i")).then_inc(ld_m, 16)
            sp.dma_start(wd[:, :, :], Wd.rearrange("(p e) i d -> (e i) p d", e=2)).then_inc(ld_m, 16)
            sp.dma_start(wgs[:, :], Wg_s).then_inc(ld_m, 16)
            sp.dma_start(wus[:, :], Wu_s).then_inc(ld_m, 16)
            sp.dma_start(wds[:, :], Wd_s).then_inc(ld_m, 16)
            sp.dma_start(gw[:, :], gate_wT).then_inc(ld_m, 16)
            sp.dma_start(cb[:, :], cbias.rearrange("(a e) -> a e", a=1).broadcast_to([P, E])).then_inc(ld_m, 16)
            for b in range(B):
                cols = slice(b * N, (b + 1) * N)
                sp.wait_ge(ql_ready, HP * (b + 1))
                if b >= 2:
                    sp.wait_ge(s_ready, 2 * HP * (b - 1))
                sp.dma_start(qb[0:DH, b % 2, :, :], qa[0:DH, :, cols]).then_inc(qb_ready, 16)
                sp.wait_ge(cT_ready, b + 1)
                sp.dma_start(qb[DH:DH + 1, b % 2, :, :], cT[:, b, :]).then_inc(crow_ready, 16)
            o_t = out.rearrange("b (t p) d -> p (b t) d", p=P)
            for t in range(XT):
                sp.wait_ge(out_ready, t + 1)
                sp.dma_start(o_t[:, t, :], outt[:, t, :]).then_inc(stored, 16)
            sp.wait_ge(stored, 16 * XT)

        @block.gpsimd
        def _(pool):
            nc.gpsimd.dma_start(lnp[:, 0:1], ln_g.rearrange("(d a) -> d a", a=1)).then_inc(ld_p, 16)
            nc.gpsimd.dma_start(lnp[:, 1:2], ln_b.rearrange("(d a) -> d a", a=1)).then_inc(ld_p, 16)
            nc.gpsimd.dma_start(lnp[:, 2:3], cln_g.rearrange("(d a) -> d a", a=1)).then_inc(ld_p, 16)
            nc.gpsimd.dma_start(lnp[:, 3:4], cln_b.rearrange("(d a) -> d a", a=1)).then_inc(ld_p, 16)
            nc.gpsimd.dma_start(gates[:, 0:1], g_xattn.rearrange("(a e) -> a e", a=1).broadcast_to([P, 1])).then_inc(ld_p, 16)
            nc.gpsimd.dma_start(gates[:, 1:2], g_ffn.rearrange("(a e) -> a e", a=1).broadcast_to([P, 1])).then_inc(ld_p, 16)
            nc.gpsimd.memset(ident[:, :], 0.0).then_inc(consts, 1)
            nc.gpsimd.memset(ident16[:, :], 0.0).then_inc(consts, 1)
            nc.gpsimd.memset(lower[:, :, :], 0.0).then_inc(consts, 1)
            nc.gpsimd.memset(esel[:, :, :, :], 0.0).then_inc(consts, 1)
            nc.gpsimd.memset(vm[:, :, DH:DH + 1], 1.0).then_inc(consts, 1)
            pool.wait_ge(consts, 5)
            nc.gpsimd.memset(kb[DH:DH + 1, :], SHIFT).then_inc(consts, 1)
            pool.wait_ge(consts, 6)
            for m in (ident, ident16):
                nc.gpsimd.affine_select(out=m[:, :], in_=m[:, :], compare_op=ALU.not_equal, fill=1.0, base=0,
                                        pattern=[[-1, P]], channel_multiplier=1).then_inc(consts, 1)
            nc.gpsimd.affine_select(out=lower[:, :, :], in_=lower[:, :, :], compare_op=ALU.is_ge, fill=1.0, base=0,
                                    pattern=[[-1, E], [1, E]], channel_multiplier=0).then_inc(consts, 1)
            nc.gpsimd.affine_select(out=esel[:, :, :, :], in_=esel[:, :, :, :], compare_op=ALU.not_equal, fill=1.0,
                                    base=0, pattern=[[-2, EP], [-1, 2], [0, I]], channel_multiplier=1).then_inc(consts, 1)
            for item in order:
                if item[0] == "S":
                    n = 2 * item[1] + item[2]
                    if n in pooled:
                        if n >= 4:
                            pool.wait_ge(o_ready, 2 * (item[1] - 1))
                        pool.wait_ge(ph_ready, n + 1)
                        nc.gpsimd.tensor_tensor(pl[:, n % 4, :], p32[:, n % 4, :], ph[:, n % 4, :],
                                                ALU.subtract).then_inc(pl_pool, 1)
                elif item[0] == "PV":
                    u = item[1]
                    b, hp, s = u // HP, u % HP, u % 2
                    pool.wait_ge(os_ready, u + 1)
                    if b >= 2 and hp == 0:
                        pool.wait_ge(oT_ready, 4 * (b - 1))
                    nc.gpsimd.tensor_tensor(
                        on[:, b % 2, :, 2 * hp:2 * hp + 2, :].rearrange("p t h d -> p h t d"), osum[:, s, :, :, :],
                        rden[:, s, :, :].unsqueeze(3).broadcast_to([P, 2, IT, DH]), ALU.mult).then_inc(on_ready, 1)

        @block.tensor
        def _(pe):
            def mm(o, l, r, start=True, stop=True):
                return nc.tensor.matmul(o, l, r, start=start, stop=stop)

            pe.wait_ge(consts, 10)
            for item in order:
                if item[0] == "S":
                    _, u, jp = item
                    n, b, hp = 2 * u + jp, u // HP, u % HP
                    if hp == 0 and jp == 0:
                        pe.wait_ge(qb_ready, 16 * (b + 1))
                        pe.wait_ge(crow_ready, 16 * (b + 1))
                        pe.wait_ge(kb_ready, b + 1)
                    if n >= 2:
                        pe.wait_ge(ph_ready, n - 1)
                    cols = slice(b * N, (b + 1) * N)
                    for j in range(2):
                        k0 = b * J + (2 * jp + j) * P
                        o = psS[:, 2 * (n % 2) + j, :]
                        mm(o, ka[:, k0:k0 + P], qa[:, 2 * hp:2 * hp + 2, cols], stop=False)
                        last = mm(o, kb[:, k0:k0 + P], qb[:, b % 2, 2 * hp:2 * hp + 2, :], start=False)
                    last.then_inc(s_ready, 1)
                elif item[0] == "PV":
                    u = item[1]
                    b, hp, s = u // HP, u % HP, u % 2
                    wait_split(pe, 2 * u)
                    wait_split(pe, 2 * u + 1)
                    pe.wait_ge(ph_ready, 2 * u + 2)
                    pe.wait_ge(vl_ready, b + 1)
                    if u >= 1:
                        pe.wait_ge(os_ready, u)
                    for h in range(2):
                        for it in range(IT):
                            o = psO[:, h, it * VW:(it + 1) * VW]
                            for jt in range(JT):
                                n = 2 * s + jt // 2
                                c0 = (jt % 2) * CH + h * N + it * P
                                v = vm[:, JT * b + jt, :]
                                mm(o, ph[:, n, c0:c0 + P], v, start=(jt == 0), stop=False)
                                last = mm(o[:, 0:DH + 1], pl[:, n, c0:c0 + P], v[:, 0:DH + 1],
                                          start=False, stop=(jt == JT - 1))
                        last.then_inc(o_ready, 1)
                else:
                    n = item[1]
                    t = tasks[n]
                    o = mbank(n)
                    if n >= 2:
                        pe.wait_ge(*m_read(n - 2))
                    b = t[1]
                    if t[0] == "XT":
                        pe.wait_ge(z_ready, 2 if b == 0 else 4)
                        for i in range(IT):
                            last = nc.tensor.transpose(o[:, i * P:(i + 1) * P], yx[:, IT * b + i, :], ident[:, :])
                    elif t[0] == "CT":
                        pe.wait_ge(z_ready, 1 if b == 0 else 3)
                        for i in range(JT):
                            last = nc.tensor.transpose(o[:, i * P:(i + 1) * P], cs[:, JT * b + i, :], ident[:, :])
                    elif t[0] == "K":
                        if b == 0:
                            pe.wait_ge(ld_k, 48)
                        pe.wait_ge(cnT_ready, b + 1)
                        last = mm(o, wkk[:, :], cnT[:, b * J:(b + 1) * J])
                    elif t[0] == "V":
                        pe.wait_ge(cnT_ready, b + 1)
                        for i in range(JT):
                            k0 = b * J + i * P
                            last = mm(o[:, i * DH:(i + 1) * DH], cnT[:, k0:k0 + P], wv[:, :])
                    elif t[0] == "Q":
                        if b == 0:
                            pe.wait_ge(ld_q, 16)
                        pe.wait_ge(xnT_ready, b + 1)
                        last = mm(o[:, 0:N], wq[:, t[2] * P:(t[2] + 1) * P], xnT[:, b * N:(b + 1) * N])
                    elif t[0] == "M":
                        _, _, h, it = t
                        pe.wait_ge(ka_ready, b + 1)
                        pe.wait_ge(ql_ready, HP * b + h // 2 + 1)
                        c0 = b * N + it * P
                        last = mm(o, qa[:, h, c0:c0 + P], ka[:, b * J:(b + 1) * J])
                    elif t[0] == "C":
                        pe.wait_ge(c16_ready, b + 1)
                        o16 = o.bitcast(F16)
                        for it in range(IT):
                            last = nc.tensor.transpose(o16[0:H, it * P:(it + 1) * P], c16[:, b, it, :], ident16[:, :])
                    elif t[0] == "F":
                        _, ft, c, half = t
                        pe.wait_ge(ld_f, 16)
                        pe.wait_ge(xnT_ready, (c + 1) * CH // N)
                        f0 = (FF if half == 0 else 0) + ft * P
                        last = mm(o, wf1[:, f0:f0 + P], xnT[:, c * CH:(c + 1) * CH])
                    elif t[0] == "T":
                        _, _, it, half = t
                        pe.wait_ge(on_ready, HP * (b + 1))
                        for i in range(4):
                            hp = 4 * half + i
                            last = nc.tensor.transpose(
                                o[:, i * P:(i + 1) * P],
                                on[:, b % 2, it, 2 * hp:2 * hp + 2, :].rearrange("p h d -> p (h d)"), ident[:, :])
                    elif t[0] == "W":
                        tt = t[1]
                        pe.wait_ge(oT_ready, 2 * (tt + 1))
                        pe.wait_ge(ff_ready, FT * NCH)
                        pe.wait_ge(ld_o, 32)
                        cols = slice(tt * P, (tt + 1) * P)
                        for ft in range(FT):
                            mm(o[:, 0:DIM], ffT[:, ft, cols], wf2[:, ft, :], start=(ft == 0), stop=False)
                        for hp in range(HP):
                            last = mm(o[:, 0:DIM], oT[:, hp, tt // IT % 2, (tt % IT) * P:(tt % IT + 1) * P], wo[:, hp, :], start=False, stop=(hp == HP - 1))
                    last.then_inc(m_ready[n % 2], 1)

            pe.wait_ge(ld_m, 128)
            for n, t in enumerate(tail):
                k, o, c = n % 8, banks[n % 8], t[1]
                if n >= 8:
                    pe.wait_ge(*t_read(n - 8))
                elif k < 2:
                    pe.wait_ge(*m_read(max(i for i in range(len(tasks)) if i % 2 == k)))
                elif k < 6:
                    pe.wait_ge(ph_ready, CHUNKS)
                else:
                    pe.wait_ge(os_ready, UNITS)
                cols = slice(c * CH, (c + 1) * CH)
                if t[0] == "YT":
                    pe.wait_ge(y2_ready, c + 1)
                    for i in range(TPC):
                        last = nc.tensor.transpose(o[:, i * P:(i + 1) * P], yx[:, TPC * c + i, :], ident[:, :])
                elif t[0] == "L":
                    pe.wait_ge(y2T_ready, c + 1)
                    for i in range(TPC):
                        t0 = c * CH + i * P
                        last = mm(o[:, i * E:(i + 1) * E], y2T[:, t0:t0 + P], gw[:, :])
                elif t[0] in ("EG", "EU"):
                    p = t[2]
                    w = (wg if t[0] == "EG" else wu)[:, 2 * p:2 * p + 2, :].rearrange("h e i -> h (e i)") if p < EP \
                        else (wgs if t[0] == "EG" else wus)[:, :]
                    last = mm(o[0:(P if p < EP else I), :], w, y2T[:, cols])
                elif t[0] == "CWT":
                    pe.wait_ge(cw_ready, c + 1)
                    for i in range(TPC):
                        last = nc.tensor.transpose(o[0:E, i * P:(i + 1) * P], cw[:, i, :], ident[:, :])
                elif t[0] == "CB":
                    pe.wait_ge(cwT_ready, c + 1)
                    last = mm(o, esel[:, t[2], :, :].rearrange("k e i -> k (e i)"), cwT[:, c, :])
                else:
                    tt = t[1]
                    c = tt // TPC
                    pe.wait_ge(hE_ready, (2 * EP + 1) * (c + 1))
                    tc = slice(tt * P, (tt + 1) * P)
                    for p in range(EP):
                        mm(o[:, 0:DIM], hE[:, p, tc], wd[:, p, :], start=(p == 0), stop=False)
                    last = mm(o[:, 0:DIM], hE[0:I, EP, tc], wds[:, :], start=False)
                last.then_inc(t_ready[k], 1)

        @block.scalar
        def _(act):
            for g in range(2):
                lo, hi = (0, 1) if g == 0 else (1, B)
                act.wait_ge(var_ready, 2 * g + 1)
                nc.scalar.activation(rstd[:, XT + JT * lo:XT + JT * hi], rstd2[:, XT + JT * lo:XT + JT * hi],
                                     ACT.Sqrt)
                nc.scalar.activation(rstd[:, IT * lo:IT * hi], rstd2[:, IT * lo:IT * hi], ACT.Sqrt).then_inc(std_ready, 1)
                act.wait_ge(var_ready, 2 * g + 2)
                nc.scalar.activation(rstd[:, IT * lo:IT * hi], rstd2[:, IT * lo:IT * hi], ACT.Sqrt).then_inc(std_ready, 1)
            act.wait_ge(ld_p, 96)
            nc.scalar.activation(tg[:, :], gates[:, :], ACT.Tanh).then_inc(tg_ready, 1)
            for item in order:
                if item[0] == "S":
                    _, u, jp = item
                    n = 2 * u + jp
                    act.wait_ge(s_ready, n + 1)
                    if n >= 4:
                        wait_split(act, n - 4)
                        act.wait_ge(o_ready, 2 * (u - 1))
                    src = psS[:, 2 * (n % 2):2 * (n % 2) + 2, :]
                    nc.scalar.activation(p32[:, n % 4, :].rearrange("p (j c) -> p j c", j=2), src, ACT.Exp,
                                         scale=SM_SCALE).then_inc(p32_ready, 1)
                    nc.scalar.activation(ph[:, n % 4, :].rearrange("p (j c) -> p j c", j=2), src, ACT.Exp,
                                         scale=SM_SCALE).then_inc(ph_ready, 1)
                elif item[0] == "PV":
                    u = item[1]
                    act.wait_ge(o_ready, 2 * (u + 1))
                    if u >= 2:
                        act.wait_ge(os_ready, u - 1)
                    nc.scalar.activation(olow[:, u % 2, :, :, :],
                                         psO[:, :, 0:IT * VW].rearrange("p h (t w) -> p h t w", w=VW)[:, :, :, DH + 1:VW],
                                         ACT.Copy).then_inc(ol_ready, 1)
                else:
                    n = item[1]
                    t = tasks[n]
                    o, b = mbank(n), t[1]
                    ready = (m_ready[n % 2], n // 2 + 1)
                    if t[0] == "CT":
                        act.wait_ge(*ready)
                        nc.scalar.activation(cnT[:, b * J:(b + 1) * J], o, ACT.Identity, bias=lnp[:, 3:4],
                                             scale=lnp[:, 2:3]).then_inc(cnT_ready, 1)
                    elif t[0] == "K":
                        act.wait_ge(*ready)
                        nc.scalar.activation(ka[:, b * J:(b + 1) * J], o, ACT.Copy).then_inc(ka_ready, 1)
                    elif t[0] == "V":
                        act.wait_ge(*ready)
                        nc.scalar.activation(vm[:, JT * b:JT * (b + 1), 0:DH],
                                             o[:, 0:JT * DH].rearrange("p (t d) -> p t d", d=DH),
                                             ACT.Copy).then_inc(vh_ready, 1)
                    elif t[0] == "Q":
                        p = t[2]
                        act.wait_ge(*ready)
                        cols = slice(b * N, (b + 1) * N)
                        nc.scalar.activation(qa[0:DH, 2 * p, cols], o[0:DH, 0:N], ACT.Copy).then_inc(qh_ready, 1)
                        nc.scalar.activation(qa[0:DH, 2 * p + 1, cols], o[DH:P, 0:N], ACT.Copy).then_inc(qh_ready, 1)
                    elif t[0] == "F" and t[3] == 0:
                        act.wait_ge(*ready)
                        k = count("F", tasks, n) // 2
                        if k >= 2:
                            act.wait_ge(ff_ready, k - 1)
                        nc.scalar.activation(sg[:, k % 2, :], o, ACT.Silu).then_inc(sg_ready, 1)
                    elif t[0] == "T":
                        _, _, it, half = t
                        act.wait_ge(*ready)
                        if b >= 2:
                            act.wait_ge(x1_ready, IT * (b - 1))
                        nc.scalar.activation(oT[:, 4 * half:4 * half + 4, b % 2, it * P:(it + 1) * P],
                                             o.rearrange("p (h c) -> p h c", h=4),
                                             ACT.Copy).then_inc(oT_ready, 1)
            for c in range(NCH):
                act.wait_ge(var2_ready, c + 1)
                nc.scalar.activation(rstd[:, TPC * c:TPC * (c + 1)], rstd2[:, TPC * c:TPC * (c + 1)],
                                     ACT.Sqrt).then_inc(std2_ready, 1)
            for n, t in enumerate(tail):
                k, o, c = n % 8, banks[n % 8], t[1]
                if t[0] == "L":
                    act.wait_ge(t_ready[k], n // 8 + 1)
                    if c >= 1:
                        act.wait_ge(cw_ready, c)
                    nc.scalar.activation(es[:, :, :], o[:, 0:TPC * E].rearrange("p (t e) -> p t e", e=E), ACT.Exp,
                                         scale=-1.0).then_inc(es_ready, 1)
                elif t[0] == "EG":
                    act.wait_ge(t_ready[k], n // 8 + 1)
                    g = c * (EP + 1) + t[2]
                    if g >= 2:
                        act.wait_ge(hE_ready, hE_at[("EU", (g - 2) // (EP + 1), (g - 2) % (EP + 1))])
                    else:
                        act.wait_ge(ff_ready, FT * NCH)
                    rows = P if t[2] < EP else I
                    nc.scalar.activation(sg[0:rows, g % 2, :], o[0:rows, :], ACT.Silu).then_inc(sg_ready, 1)
                elif t[0] == "CWT":
                    act.wait_ge(t_ready[k], n // 8 + 1)
                    nc.scalar.activation(cwT[:, c, :], o[0:E, :], ACT.Copy).then_inc(cwT_ready, 1)

        @block.vector
        def _(dve):
            done = [0]

            def step(ins):
                done[0] += 1
                ins.then_inc(chain, 1)
                dve.wait_ge(chain, done[0])

            def statistics(tiles):
                for i, src in tiles:
                    last = nc.vector.bn_stats(stats[:, i, :], src)
                step(last)
                for i, _ in tiles:
                    last = nc.vector.bn_aggr(mv[:, i, :], stats[:, i, :])
                step(last)

            for g in range(2):
                lo, hi = (0, 1) if g == 0 else (1, B)
                for b in range(lo, hi):
                    dve.wait_ge(ld_c[b], 16)
                    dve.wait_ge(ld_x[b], 16)
                xt = list(range(IT * lo, IT * hi))
                ct = list(range(JT * lo, JT * hi))
                x_r, c_r = slice(IT * lo, IT * hi), slice(XT + JT * lo, XT + JT * hi)
                statistics([(i, xs[:, i, :]) for i in xt] + [(XT + i, cs[:, i, :]) for i in ct])
                nc.vector.tensor_scalar(rstd2[:, c_r], mv[:, c_r, 1], EPS, None, ALU.add)
                nc.vector.tensor_scalar(rstd2[:, x_r], mv[:, x_r, 1], EPS, None, ALU.add).then_inc(var_ready, 1)
                dve.wait_ge(std_ready, 2 * g + 1)
                nc.vector.reciprocal(rstd2[:, c_r], rstd[:, c_r])
                step(nc.vector.reciprocal(rstd2[:, x_r], rstd[:, x_r]))
                for i in xt:
                    last = nc.vector.tensor_scalar(yx[:, i, :], xs[:, i, :], mv[:, i, 0:1], rstd2[:, i:i + 1],
                                                   ALU.subtract, ALU.mult)
                step(last)
                statistics([(i, yx[:, i, :]) for i in xt])
                nc.vector.tensor_scalar(rstd2[:, x_r], mv[:, x_r, 1], EPS, None, ALU.add).then_inc(var_ready, 1)
                for i in ct:
                    last = nc.vector.tensor_scalar(cs[:, i, :], cs[:, i, :], mv[:, XT + i, 0:1],
                                                   rstd2[:, XT + i:XT + i + 1], ALU.subtract, ALU.mult)
                last.then_inc(z_ready, 1)
                dve.wait_ge(std_ready, 2 * g + 2)
                step(nc.vector.reciprocal(rstd2[:, x_r], rstd[:, x_r]))
                for i in xt:
                    last = nc.vector.tensor_scalar(yx[:, i, :], yx[:, i, :], mv[:, i, 0:1], rstd2[:, i:i + 1],
                                                   ALU.subtract, ALU.mult)
                last.then_inc(z_ready, 1)
            dve.wait_ge(ld_p, 96)

            for item in order:
                if item[0] == "S":
                    n = 2 * item[1] + item[2]
                    if n not in pooled:
                        if n >= 4:
                            dve.wait_ge(o_ready, 2 * (item[1] - 1))
                        dve.wait_ge(ph_ready, n + 1)
                        nc.vector.tensor_tensor(pl[:, n % 4, :], p32[:, n % 4, :], ph[:, n % 4, :],
                                                ALU.subtract).then_inc(pl_dve, 1)
                elif item[0] == "PV":
                    u = item[1]
                    s = u % 2
                    dve.wait_ge(ol_ready, u + 1)
                    if u >= 2:
                        dve.wait_ge(on_ready, u - 1)
                    o = psO[:, :, 0:IT * VW].rearrange("p h (t w) -> p h t w", w=VW)
                    nc.vector.reciprocal(rden[:, s, :, :], o[:, :, :, DH]).then_inc(rden_ready, 1)
                    nc.vector.tensor_tensor(osum[:, s, :, :, :], o[:, :, :, 0:DH], olow[:, s, :, :, :],
                                            ALU.add).then_inc(os_ready, 1)
                else:
                    n = item[1]
                    t = tasks[n]
                    o, b = mbank(n), t[1]
                    ready = (m_ready[n % 2], n // 2 + 1)
                    if t[0] == "XT":
                        dve.wait_ge(*ready)
                        nc.vector.tensor_scalar(xnT[:, b * N:(b + 1) * N], o[:, 0:N], lnp[:, 0:1], lnp[:, 1:2],
                                                ALU.mult, ALU.add).then_inc(xnT_ready, 1)
                    elif t[0] == "K":
                        dve.wait_ge(ka_ready, b + 1)
                        cols = slice(b * J, (b + 1) * J)
                        nc.vector.tensor_tensor(kb[0:DH, cols], o[0:DH, :], ka[0:DH, cols],
                                                ALU.subtract).then_inc(kb_ready, 1)
                    elif t[0] == "V":
                        dve.wait_ge(vh_ready, b + 1)
                        nc.vector.tensor_tensor(vm[:, JT * b:JT * (b + 1), DH + 1:VW],
                                                o[:, 0:JT * DH].rearrange("p (t d) -> p t d", d=DH),
                                                vm[:, JT * b:JT * (b + 1), 0:DH],
                                                ALU.subtract).then_inc(vl_ready, 1)
                    elif t[0] == "Q":
                        p = t[2]
                        dve.wait_ge(qh_ready, 2 * (HP * b + p + 1))
                        cols = slice(b * N, (b + 1) * N)
                        nc.vector.tensor_tensor(qa[DH:P, 2 * p, cols], o[0:DH, 0:N], qa[0:DH, 2 * p, cols], ALU.subtract)
                        nc.vector.tensor_tensor(qa[DH:P, 2 * p + 1, cols], o[DH:P, 0:N], qa[0:DH, 2 * p + 1, cols],
                                                ALU.subtract).then_inc(ql_ready, 1)
                    elif t[0] == "M":
                        _, _, h, it = t
                        dve.wait_ge(*ready)
                        nc.vector.tensor_reduce(mx[:, b, it, h:h + 1], o, AX_X,
                                                ALU.max).then_inc(mx_ready, 1)
                    elif t[0] == "C":
                        dve.wait_ge(mx_ready, H * IT * (b + 1))
                        nc.vector.tensor_scalar(c16[:, b, :, :], mx[:, b, :, :], -1.0 / SHIFT, None,
                                                ALU.mult).then_inc(c16_ready, 1)
                        dve.wait_ge(*ready)
                        nc.vector.tensor_copy(cT[:, b, :], o.bitcast(F16)[0:H, 0:N]).then_inc(cT_ready, 1)
                    elif t[0] == "F" and t[3] == 1:
                        _, ft, c, _ = t
                        k = count("F", tasks, n) // 2
                        dve.wait_ge(sg_ready, k + 1)
                        dve.wait_ge(*ready)
                        nc.vector.tensor_tensor(ffT[:, ft, c * CH:(c + 1) * CH], o, sg[:, k % 2, :],
                                                ALU.mult).then_inc(ff_ready, 1)
                    elif t[0] == "W":
                        tt = t[1]
                        dve.wait_ge(*ready)
                        dve.wait_ge(tg_ready, 1)
                        nc.vector.scalar_tensor_tensor(x1[:, tt, :], o[:, 0:DIM], tg[:, 0:1], xs[:, tt, :],
                                                       ALU.mult, ALU.add).then_inc(x1_ready, 1)

            for c in range(NCH):
                ts = list(range(TPC * c, TPC * (c + 1)))
                r = slice(TPC * c, TPC * (c + 1))
                dve.wait_ge(x1_ready, TPC * (c + 1))
                statistics([(i, x1[:, i, :]) for i in ts])
                nc.vector.tensor_scalar(rstd2[:, r], mv[:, r, 1], EPS, None, ALU.add).then_inc(var2_ready, 1)
            for c in range(NCH):
                ts = list(range(TPC * c, TPC * (c + 1)))
                r = slice(TPC * c, TPC * (c + 1))
                dve.wait_ge(std2_ready, c + 1)
                step(nc.vector.reciprocal(rstd2[:, r], rstd[:, r]))
                for i in ts:
                    last = nc.vector.tensor_scalar(yx[:, i, :], x1[:, i, :], mv[:, i, 0:1], rstd2[:, i:i + 1],
                                                   ALU.subtract, ALU.mult)
                last.then_inc(y2_ready, 1)

            def route(c):
                pair = [P, TPC, E, E]
                gpair = [P, TPC, NG, NG]
                dve.wait_ge(es_ready, c + 1)
                step(nc.vector.tensor_scalar(es[:, :, :], es[:, :, :], 1.0, None, ALU.add))
                step(nc.vector.reciprocal(sc[:, :, :], es[:, :, :]))
                step(nc.vector.tensor_tensor(scc[:, :, :], sc[:, :, :],
                                             cb[:, :].unsqueeze(1).broadcast_to([P, TPC, E]), ALU.add))
                step(nc.vector.tensor_reduce(grp[:, :, :], scc[:, :, :].rearrange("p t (g m) -> p t g m", m=EPG),
                                             AX_X, ALU.add))
                other, own = grp[:, :, :].unsqueeze(2).broadcast_to(gpair), grp[:, :, :].unsqueeze(3).broadcast_to(gpair)
                a, bb = cmpA[:, :, 0:NG, 0:NG], cmpB[:, :, 0:NG, 0:NG]
                nc.vector.tensor_tensor(a, other, own, ALU.is_gt)
                step(nc.vector.tensor_tensor(bb, other, own, ALU.is_equal))
                step(nc.vector.tensor_tensor(bb, bb, lower[:, 0:NG, 0:NG].unsqueeze(1).broadcast_to(gpair), ALU.mult))
                step(nc.vector.tensor_tensor(a, a, bb, ALU.add))
                step(nc.vector.tensor_reduce(grank[:, :, :], a, AX_X, ALU.add))
                step(nc.vector.tensor_scalar(gsel[:, :, :], grank[:, :, :], float(TKG), None, ALU.is_lt))
                step(nc.vector.tensor_tensor(choice[:, :, :].rearrange("p t (g m) -> p t g m", m=EPG),
                                             scc[:, :, :].rearrange("p t (g m) -> p t g m", m=EPG),
                                             gsel[:, :, :].unsqueeze(3).broadcast_to([P, TPC, NG, EPG]), ALU.mult))
                other, own = choice[:, :, :].unsqueeze(2).broadcast_to(pair), choice[:, :, :].unsqueeze(3).broadcast_to(pair)
                nc.vector.tensor_tensor(cmpA[:, :, :, :], other, own, ALU.is_gt)
                step(nc.vector.tensor_tensor(cmpB[:, :, :, :], other, own, ALU.is_equal))
                step(nc.vector.tensor_tensor(cmpB[:, :, :, :], cmpB[:, :, :, :],
                                             lower[:, :, :].unsqueeze(1).broadcast_to(pair), ALU.mult))
                step(nc.vector.tensor_tensor(cmpA[:, :, :, :], cmpA[:, :, :, :], cmpB[:, :, :, :], ALU.add))
                step(nc.vector.tensor_reduce(rank[:, :, :], cmpA[:, :, :, :], AX_X, ALU.add))
                step(nc.vector.tensor_scalar(rank[:, :, :], rank[:, :, :], float(TOPK), None, ALU.is_lt))
                step(nc.vector.tensor_tensor(sc[:, :, :], sc[:, :, :], rank[:, :, :], ALU.mult))
                step(nc.vector.tensor_reduce(wsum[:, :], sc[:, :, :], AX_X, ALU.add))
                step(nc.vector.tensor_scalar(wsum[:, :], wsum[:, :], 1e-20, None, ALU.add))
                step(nc.vector.reciprocal(wsum[:, :], wsum[:, :]))
                step(nc.vector.tensor_scalar(wsum[:, :], wsum[:, :], ROUTE_SCALE, None, ALU.mult))
                if c >= 1:
                    dve.wait_ge(cwT_ready, c)
                nc.vector.tensor_tensor(cw[:, :, :], sc[:, :, :], wsum[:, :].unsqueeze(2).broadcast_to([P, TPC, E]),
                                        ALU.mult).then_inc(cw_ready, 1)

            for n, t in enumerate(tail):
                k, o, c = n % 8, banks[n % 8], t[1]
                ready = (t_ready[k], n // 8 + 1)
                cols = slice(c * CH, (c + 1) * CH)
                if t[0] == "YT":
                    dve.wait_ge(*ready)
                    nc.vector.tensor_copy(y2T[:, cols], o).then_inc(y2T_ready, 1)
                elif t[0] == "L":
                    if c == 1:
                        continue
                    route(c)
                elif t[0] == "EU":
                    g = c * (EP + 1) + t[2]
                    rows = P if t[2] < EP else I
                    dve.wait_ge(sg_ready, FT * NCH + g + 1)
                    dve.wait_ge(*ready)
                    last = nc.vector.tensor_tensor(hE[0:rows, t[2], cols], o[0:rows, :], sg[0:rows, g % 2, :], ALU.mult)
                    last.then_inc(hE_ready, 1)
                    if c == 0 and t[2] == EP:
                        route(1)
                elif t[0] == "CB":
                    dve.wait_ge(*ready)
                    dve.wait_ge(hE_ready, hE_at[("EU", c, t[2])])
                    last = nc.vector.tensor_tensor(hE[:, t[2], cols], hE[:, t[2], cols], o, ALU.mult)
                    last.then_inc(hE_ready, 1)
                elif t[0] == "D":
                    dve.wait_ge(*ready)
                    nc.vector.scalar_tensor_tensor(outt[:, t[1], :], o[:, 0:DIM], tg[:, 1:2], x1[:, t[1], :],
                                                   ALU.mult, ALU.add).then_inc(out_ready, 1)


_INS = ["x", "ctx_1024", "g_xattn", "g_ffn", "L0_xattn_ln_g", "L0_xattn_ln_b", "L0_xattn_cln_g", "L0_xattn_cln_b",
        "L0_xattn_Wq", "L0_xattn_Wkv", "L0_xattn_Wo", "L0_xattn_Wff1", "L0_xattn_Wff2", "L0_ffn_gate_w",
        "L0_ffn_correction_bias", "L0_ffn_Wg", "L0_ffn_Wu", "L0_ffn_Wd", "L0_ffn_Wg_s", "L0_ffn_Wu_s", "L0_ffn_Wd_s"]


def kernel(**inputs):
    import numpy as _np
    import concourse.bacc as _bacc
    from concourse import mybir as _mybir
    from concourse.bass_utils import run_bass_kernel_spmd as _run

    nc = _bacc.Bacc("TRN2", target_bir_lowering=False, num_devices=1)
    arrays, args = {}, []
    for name in _INS:
        a = _np.asarray(inputs[name])
        if name == "L0_ffn_gate_w":
            a = a.T
        a = _np.ascontiguousarray(a)
        arrays[f"in_{name}"] = a
        args.append(nc.dram_tensor(f"in_{name}", a.shape, _mybir.dt.from_np(a.dtype), kind="ExternalInput").ap())
    shape = _np.asarray(inputs["x"]).shape
    args.append(nc.dram_tensor("out_x", shape, _mybir.dt.float32, kind="ExternalOutput").ap())
    flamingo_gated_moe(nc, *args)
    r = _run(nc, [arrays], core_ids=[0])
    return r.results[0]["out_x"]
```

```python
from contextlib import ExitStack

import concourse.bass as bass
from concourse import mybir

P = 128
F32 = mybir.dt.float32
F16 = mybir.dt.float16
ALU = mybir.AluOpType
ACT = mybir.ActivationFunctionType
AX_X = mybir.AxisListType.X


def flamingo_gated_moe(nc, x, ctx_in, g_xattn, g_ffn, ln_g, ln_b, cln_g, cln_b, Wq, Wkv, Wo, Wff1, Wff2,
                       gate_wT, cbias, Wg, Wu, Wd, Wg_s, Wu_s, Wd_s, out):
    B, N, DIM = x.shape
    J = ctx_in.shape[1]
    INNER = Wq.shape[1]
    DH = Wkv.shape[1] // 2
    H = INNER // DH
    FF = Wff2.shape[0]
    E, _, I = Wg.shape
    NG, TKG, TOPK, ROUTE_SCALE = 4, 2, 4, 2.5
    EPG = E // NG
    assert DIM == P and 2 * DH == P and 2 * I == P and J % P == 0 and N % P == 0
    EPS = 1e-5
    SM_SCALE = DH ** -0.5
    SHIFT = 16.0
    TOK = B * N
    XT = TOK // P
    CT = B * J // P
    IT = N // P
    JT = J // P
    HP = H // 2
    FT = FF // P
    EP = E // 2
    CH = 512
    NCH = TOK // CH
    TPC = CH // P
    VW = 2 * DH + 1
    MB = 3
    OW = DH + 1
    UNITS = B * HP
    CHUNKS = 2 * UNITS
    PSLOTS = 6
    LAG = 2
    LEAD = 5
    QLEAD = LEAD + 2
    HALF = HP // 2

    with ExitStack() as stack:
        def sb(name, shape, dt=F32):
            return stack.enter_context(nc.sbuf_tensor(name, shape, dt))

        def sem(name):
            return stack.enter_context(nc.semaphore(name))

        psM = stack.enter_context(nc.psum_tensor("psM", [P, MB, 512], F32))
        psS = stack.enter_context(nc.psum_tensor("psS", [P, 4, 512], F32))
        psO = stack.enter_context(nc.psum_tensor("psO", [P, 512], F32))

        xs = sb("xs", [P, XT, DIM])
        yx = sb("yx", [P, XT, DIM])
        cs = sb("cs", [P, CT, DIM])
        stats = sb("stats", [P, XT + CT, 6])
        mv = sb("mv", [P, XT + CT, 2])
        rstd = sb("rstd", [P, XT + CT])
        rstd2 = sb("rstd2", [P, XT + CT])
        xnT = sb("xnT", [P, TOK])
        cnT = sb("cnT", [P, B * J])
        wq = sb("wq", [P, INNER])
        wkk = sb("wkk", [P, 2 * DH])
        wv = sb("wv", [P, DH])
        wo = sb("wo", [P, HP, DIM])
        wf1 = sb("wf1", [P, 2 * FF])
        wf2 = sb("wf2", [P, FT, DIM])
        wg = sb("wg", [P, E, I])
        wu = sb("wu", [P, E, I])
        wd = sb("wd", [P, EP, DIM])
        wgs = sb("wgs", [P, I])
        wus = sb("wus", [P, I])
        wds = sb("wds", [I, DIM])
        gw = sb("gw", [P, E])
        cb = sb("cb", [P, E])
        lnp = sb("lnp", [P, 4])
        gates = sb("gates", [P, 2])
        tg = sb("tg", [P, 2])
        ident = sb("ident", [P, P])
        ident16 = sb("ident16", [P, P], F16)
        lower = sb("lower", [P, E, E])
        esel = sb("esel", [E, EP, 2, I])
        qa = sb("qa", [P, 2, H, N], F16)
        qb = sb("qb", [DH + 1, 2, H, N], F16)
        ka = sb("ka", [P, B * J], F16)
        kb = sb("kb", [DH + 1, B * J], F16)
        vm = sb("vm", [P, CT, VW], F16)
        mx = sb("mx", [P, B, IT, H])
        c16 = sb("c16", [P, B, IT, H], F16)
        cT = sb("cT", [H // 2, B, 2, N], F16)
        p32 = sb("p32", [P, 4, 2 * CH])
        ph = sb("ph", [P, PSLOTS, 2 * CH], F16)
        pl = sb("pl", [P, PSLOTS, 2 * CH], F16)
        rden = sb("rden", [P, 2, 2, IT])
        on = sb("on", [P, 2, IT, H, DH])
        oT = sb("oT", [P, HP, 2, N])
        sg = sb("sg", [P, 2, CH])
        ffT = sb("ffT", [P, FT, TOK])
        x1 = xs
        y2T = xnT
        def hE(p):
            return ffT[:, p, :] if p < EP else oT[:, 0:TOK // (2 * N), :, :].rearrange("p h b t -> p (h b t)")

        es = sb("es", [P, TPC, E])
        sc = sb("sc", [P, TPC, E])
        scc = sb("scc", [P, TPC, E])
        grp = sb("grp", [P, TPC, NG])
        cmpA = p32[:, 0, 0:TPC * E * E].rearrange("p (t e f) -> p t e f", e=E, f=E)
        cmpB = p32[:, 1, 0:TPC * E * E].rearrange("p (t e f) -> p t e f", e=E, f=E)
        gsel = sb("gsel", [P, TPC, NG])
        choice = sb("choice", [P, TPC, E])
        rank = sb("rank", [P, TPC, E])
        grank = sb("grank", [P, TPC, NG])
        wsum = sb("wsum", [P, TPC])
        cw = sb("cw", [P, TPC, E])
        cwT = p32[0:E, 2, :].rearrange("e (c t) -> e c t", c=NCH)
        outt = cs

        ld_x = [sem(f"ld_x{b}") for b in range(B)]
        ld_c = [sem(f"ld_c{b}") for b in range(B)]
        ld_p = sem("ld_p")
        ld_k, ld_q = sem("ld_k"), sem("ld_q")
        ld_f, ld_o, ld_m = sem("ld_f"), sem("ld_o"), sem("ld_m")
        consts = sem("consts")
        chain = sem("chain")
        tg_ready = sem("tg_ready")
        var_ready = sem("var_ready")
        std_ready = sem("std_ready")
        rs_ready = sem("rs_ready")
        zc_ready, zx_ready = sem("zc_ready"), sem("zx_ready")
        m_ready = [sem(f"m_ready{i}") for i in range(MB)]
        xnT_ready, cnT_ready = sem("xnT_ready"), sem("cnT_ready")
        ka_ready, kb_ready = sem("ka_ready"), sem("kb_ready")
        vh_ready, vl_ready = sem("vh_ready"), sem("vl_ready")
        ql_ready = sem("ql_ready")
        qb_ready = sem("qb_ready")
        mx_ready = sem("mx_ready")
        c16_ready, cT_ready, crow_ready = sem("c16_ready"), sem("cT_ready"), sem("crow_ready")
        s_ready = sem("s_ready")
        ph_ready = sem("ph_ready")
        p32_ready = sem("p32_ready")
        pl_dve, pl_pool = sem("pl_dve"), sem("pl_pool")
        o_ready, on_ready = sem("o_ready"), sem("on_ready")
        oT_ready = sem("oT_ready")
        sg_ready, ff_ready = sem("sg_ready"), sem("ff_ready")
        x1_ready = sem("x1_ready")
        var2_ready, std2_ready = sem("var2_ready"), sem("std2_ready")
        y2_ready, y2T_ready = sem("y2_ready"), sem("y2T_ready")
        t_ready = [sem(f"t_ready{i}") for i in range(8)]
        es_ready, cw_ready, cwT_ready = sem("es_ready"), sem("cw_ready"), sem("cwT_ready")
        hE_ready = sem("hE_ready")
        out_ready, stored = sem("out_ready"), sem("stored")

        tasks, order = [], []

        def task(*t):
            order.append(("task", len(tasks)))
            tasks.append(t)

        def maxima(u):
            b, hp = u // HP, u % HP
            return [("M", b, 2 * hp + h, it) for h in range(2) for it in range(IT)]

        def after_maxima(u):
            return [("C", u // HP, u % HP // HALF)] if u % HALF == HALF - 1 else []

        order.append(("LN", 0))
        task("XT", 0)
        task("CT", 0)
        task("K", 0)
        for p in range(2):
            task("Q", 0, p)
        order.append(("LN", 1))
        for p in range(2, QLEAD):
            task("Q", 0, p)
        task("V", 0)
        for b in range(1, B):
            task("XT", b)
            task("CT", b)
        first = [t for u in range(LEAD) for t in maxima(u) + after_maxima(u)]
        ffs = [("F", ft, c, half) for c in range(NCH) for ft in range(FT) for half in range(2)]
        while first or ffs:
            for t in first[:3]:
                task(*t)
            first = first[3:]
            for t in ffs[:2]:
                task(*t)
            ffs = ffs[2:]
        for u in range(UNITS + LAG):
            b, hp = u // HP, u % HP
            side = []
            if u + QLEAD < UNITS:
                side += [("Q", (u + QLEAD) // HP, (u + QLEAD) % HP)]
            if b + 1 < B and hp == 0:
                side = [("K", b + 1)] + side
            if b + 1 < B and hp == 1:
                side += [("V", b + 1)]
            if b >= 1 and hp in (3, 5):
                side += [("T", b - 1, hp // 4, 0), ("T", b - 1, hp // 4, 1)]
            if b >= 1 and hp in (4, 6):
                side += [("W", IT * (b - 1) + (hp - 4) // 2)]
            ms = maxima(u + LEAD) + after_maxima(u + LEAD) if u + LEAD < UNITS else []
            if u < UNITS:
                order.append(("S", u, 0))
            for t in ms[:2]:
                task(*t)
            if 1 <= u <= UNITS:
                order.append(("PL", 2 * u - 1))
            if u >= LAG:
                order.append(("PV", u - LAG, 0))
            if u < UNITS:
                order.append(("S", u, 1))
            for t in ms[2:]:
                task(*t)
            if u >= LAG:
                order.append(("PV", u - LAG, 1))
                order.append(("O", u - LAG))
            for t in side:
                task(*t)
        for it in range(IT):
            task("T", B - 1, it, 0)
            task("T", B - 1, it, 1)
            task("W", IT * (B - 1) + it)

        tail = []
        for c in range(NCH):
            tail += [("YT", c), ("L", c)]
        for c in range(NCH):
            for p in range(EP + 1):
                tail += [("EG", c, p), ("EU", c, p)]
                if p == 1:
                    tail += [("CWT", c)]
            tail += [("CB", c, p) for p in range(EP)]
            tail += [("D", c * TPC + t) for t in range(TPC)]

        def count(kind, items, upto):
            return sum(1 for t in items[:upto] if t[0] == kind)

        pool_halves = [n for n in range(CHUNKS) if n % 8 != 3]
        pooled = set(pool_halves)

        def wait_split(eng, n):
            if n in pooled:
                eng.wait_ge(pl_pool, sum(1 for m in pooled if m <= n))
            else:
                eng.wait_ge(pl_dve, n + 1 - sum(1 for m in pooled if m <= n))

        def mbank(n):
            return psM[:, n % MB, :]

        banks = [psM[:, i, :] for i in range(MB)] + [psS[:, i, :] for i in range(4)] + [psO[:, :]]

        def m_read(n):
            t = tasks[n]
            same = count(t[0], tasks, n) + 1
            if t[0] == "F":
                return (sg_ready, (same + 1) // 2) if t[3] == 0 else (ff_ready, same // 2)
            return {"XT": xnT_ready, "CT": cnT_ready, "K": kb_ready, "V": vl_ready, "Q": ql_ready, "M": mx_ready,
                    "C": cT_ready, "T": oT_ready, "W": x1_ready}[t[0]], same

        hE_at = {t: i + 1 for i, t in enumerate(t for t in tail if t[0] in ("EU", "CB"))}

        def t_read(n):
            t = tail[n]
            if t in hE_at:
                return hE_ready, hE_at[t]
            same = count(t[0], tail, n) + 1
            if t[0] == "EG":
                return sg_ready, FT * NCH + same
            return {"YT": y2T_ready, "L": es_ready, "CWT": cwT_ready, "D": out_ready}[t[0]], same

        block = stack.enter_context(nc.Block())

        @block.sync
        def _(sp):
            x_t = x.rearrange("b (t p) d -> p (b t) d", p=P)
            c_t = ctx_in.rearrange("b (t p) d -> p (b t) d", p=P)
            for b in range(B):
                sp.dma_start(xs[:, IT * b:IT * (b + 1), :], x_t[:, IT * b:IT * (b + 1), :]).then_inc(ld_x[b], 16)
                sp.dma_start(cs[:, JT * b:JT * (b + 1), :], c_t[:, JT * b:JT * (b + 1), :]).then_inc(ld_c[b], 16)
                if b == 0:
                    sp.dma_start(wkk[:, 0:DH], Wkv[:, 0:DH]).then_inc(ld_k, 16)
                    sp.dma_start(wkk[:, DH:2 * DH], Wkv[:, 0:DH]).then_inc(ld_k, 16)
                    sp.dma_start(wv[:, :], Wkv[:, DH:2 * DH]).then_inc(ld_k, 16)
                    sp.dma_start(wq[:, :], Wq).then_inc(ld_q, 16)
            sp.dma_start(wf1[:, :], Wff1).then_inc(ld_f, 16)
            sp.dma_start(wo[:, :, :], Wo.rearrange("(p r) d -> r p d", r=P)).then_inc(ld_o, 16)
            sp.dma_start(wf2[:, :, :], Wff2.rearrange("(p r) d -> r p d", r=P)).then_inc(ld_o, 16)
            sp.dma_start(wg[:, :, :], Wg.rearrange("e h i -> h e i")).then_inc(ld_m, 16)
            sp.dma_start(wu[:, :, :], Wu.rearrange("e h i -> h e i")).then_inc(ld_m, 16)
            sp.dma_start(wd[:, :, :], Wd.rearrange("(p e) i d -> (e i) p d", e=2)).then_inc(ld_m, 16)
            sp.dma_start(wgs[:, :], Wg_s).then_inc(ld_m, 16)
            sp.dma_start(wus[:, :], Wu_s).then_inc(ld_m, 16)
            sp.dma_start(wds[:, :], Wd_s).then_inc(ld_m, 16)
            sp.dma_start(gw[:, :], gate_wT).then_inc(ld_m, 16)
            sp.dma_start(cb[:, :], cbias.rearrange("(a e) -> a e", a=1).broadcast_to([P, E])).then_inc(ld_m, 16)
            for b in range(B):
                for half in range(2):
                    hs = slice(half * H // 2, (half + 1) * H // 2)
                    sp.wait_ge(ql_ready, HP * b + HALF * (half + 1))
                    if b >= 2:
                        sp.wait_ge(s_ready, 2 * (HP * (b - 2) + HALF * (half + 1)))
                    sp.dma_start(qb[0:DH, b % 2, hs, :], qa[0:DH, b % 2, hs, :]).then_inc(qb_ready, 16)
                    sp.wait_ge(cT_ready, 2 * b + half + 1)
                    sp.dma_start(qb[DH:DH + 1, b % 2, hs, :], cT[:, b, half, :]).then_inc(crow_ready, 16)
            o_t = out.rearrange("b (t p) d -> p (b t) d", p=P)
            for t in range(XT):
                sp.wait_ge(out_ready, t + 1)
                sp.dma_start(o_t[:, t, :], outt[:, t, :]).then_inc(stored, 16)
            sp.wait_ge(stored, 16 * XT)

        @block.gpsimd
        def _(pool):
            nc.gpsimd.dma_start(lnp[:, 0:1], ln_g.rearrange("(d a) -> d a", a=1)).then_inc(ld_p, 16)
            nc.gpsimd.dma_start(lnp[:, 1:2], ln_b.rearrange("(d a) -> d a", a=1)).then_inc(ld_p, 16)
            nc.gpsimd.dma_start(lnp[:, 2:3], cln_g.rearrange("(d a) -> d a", a=1)).then_inc(ld_p, 16)
            nc.gpsimd.dma_start(lnp[:, 3:4], cln_b.rearrange("(d a) -> d a", a=1)).then_inc(ld_p, 16)
            nc.gpsimd.dma_start(gates[:, 0:1], g_xattn.rearrange("(a e) -> a e", a=1).broadcast_to([P, 1])).then_inc(ld_p, 16)
            nc.gpsimd.dma_start(gates[:, 1:2], g_ffn.rearrange("(a e) -> a e", a=1).broadcast_to([P, 1])).then_inc(ld_p, 16)
            nc.gpsimd.memset(ident[:, :], 0.0).then_inc(consts, 1)
            nc.gpsimd.memset(ident16[:, :], 0.0).then_inc(consts, 1)
            nc.gpsimd.memset(lower[:, :, :], 0.0).then_inc(consts, 1)
            nc.gpsimd.memset(esel[:, :, :, :], 0.0).then_inc(consts, 1)
            nc.gpsimd.memset(vm[:, :, DH:DH + 1], 1.0).then_inc(consts, 1)
            pool.wait_ge(consts, 5)
            nc.gpsimd.memset(kb[DH:DH + 1, :], SHIFT).then_inc(consts, 1)
            pool.wait_ge(consts, 6)
            for m in (ident, ident16):
                nc.gpsimd.affine_select(out=m[:, :], in_=m[:, :], compare_op=ALU.not_equal, fill=1.0, base=0,
                                        pattern=[[-1, P]], channel_multiplier=1).then_inc(consts, 1)
            nc.gpsimd.affine_select(out=lower[:, :, :], in_=lower[:, :, :], compare_op=ALU.is_ge, fill=1.0, base=0,
                                    pattern=[[-1, E], [1, E]], channel_multiplier=0).then_inc(consts, 1)
            nc.gpsimd.affine_select(out=esel[:, :, :, :], in_=esel[:, :, :, :], compare_op=ALU.not_equal, fill=1.0,
                                    base=0, pattern=[[-2, EP], [-1, 2], [0, I]], channel_multiplier=1).then_inc(consts, 1)
            for item in order:
                if item[0] == "LN" and item[1] == 1:
                    pool.wait_ge(rs_ready, 1)
                    for i in range(JT, CT):
                        last = nc.gpsimd.tensor_scalar(cs[:, i, :], cs[:, i, :], mv[:, XT + i, 0:1],
                                                       rstd2[:, XT + i:XT + i + 1], ALU.subtract, ALU.mult)
                        if i % JT == JT - 1:
                            last.then_inc(zc_ready, 1)
                elif item[0] == "S":
                    n = 2 * item[1] + item[2]
                    if n in pooled:
                        if n >= PSLOTS:
                            pool.wait_ge(o_ready, item[1] - 2)
                        pool.wait_ge(ph_ready, n + 1)
                        nc.gpsimd.tensor_tensor(pl[:, n % PSLOTS, :], p32[:, n % 4, :], ph[:, n % PSLOTS, :],
                                                ALU.subtract).then_inc(pl_pool, 1)

        @block.tensor
        def _(pe):
            def mm(o, l, r, start=True, stop=True):
                return nc.tensor.matmul(o, l, r, start=start, stop=stop)

            pe.wait_ge(consts, 10)
            for item in order:
                if item[0] == "S":
                    _, u, jp = item
                    n, b, hp = 2 * u + jp, u // HP, u % HP
                    if hp % HALF == 0 and jp == 0:
                        pe.wait_ge(qb_ready, 16 * (2 * b + hp // HALF + 1))
                        pe.wait_ge(crow_ready, 16 * (2 * b + hp // HALF + 1))
                        pe.wait_ge(kb_ready, b + 1)
                    if n >= 2:
                        pe.wait_ge(ph_ready, n - 1)
                    for j in range(2):
                        k0 = b * J + (2 * jp + j) * P
                        o = psS[:, 2 * (n % 2) + j, :]
                        mm(o, ka[:, k0:k0 + P], qa[:, b % 2, 2 * hp:2 * hp + 2, :], stop=False)
                        last = mm(o, kb[:, k0:k0 + P], qb[:, b % 2, 2 * hp:2 * hp + 2, :], start=False)
                    last.then_inc(s_ready, 1)
                elif item[0] == "PV":
                    _, u, h = item
                    b = u // HP
                    if h == 0:
                        wait_split(pe, 2 * u)
                        wait_split(pe, 2 * u + 1)
                        pe.wait_ge(ph_ready, 2 * u + 2)
                        pe.wait_ge(vl_ready, b + 1)
                        if u >= 1:
                            pe.wait_ge(on_ready, u)
                    for it in range(IT):
                        g = (h * IT + it) * OW
                        o = psO[:, g:g + OW]
                        for jt in range(JT):
                            n = (2 * u + jt // 2) % PSLOTS
                            c0 = (jt % 2) * CH + h * N + it * P
                            v = vm[:, JT * b + jt, :]
                            mm(o, ph[:, n, c0:c0 + P], v[:, 0:OW], start=(jt == 0), stop=False)
                            mm(o[:, 0:DH], ph[:, n, c0:c0 + P], v[:, OW:VW], start=False, stop=False)
                            last = mm(o, pl[:, n, c0:c0 + P], v[:, 0:OW], start=False, stop=(jt == JT - 1))
                    if h == 1:
                        last.then_inc(o_ready, 1)
                elif item[0] in ("LN", "O", "PL"):
                    pass
                else:
                    n = item[1]
                    t = tasks[n]
                    o = mbank(n)
                    if n >= MB:
                        pe.wait_ge(*m_read(n - MB))
                    b = t[1]
                    if t[0] == "XT":
                        pe.wait_ge(zx_ready, 1 if b == 0 else 2)
                        for i in range(IT):
                            last = nc.tensor.transpose(o[:, i * P:(i + 1) * P], yx[:, IT * b + i, :], ident[:, :])
                    elif t[0] == "CT":
                        pe.wait_ge(zc_ready, b + 1)
                        for i in range(JT):
                            last = nc.tensor.transpose(o[:, i * P:(i + 1) * P], cs[:, JT * b + i, :], ident[:, :])
                    elif t[0] == "K":
                        if b == 0:
                            pe.wait_ge(ld_k, 48)
                        pe.wait_ge(cnT_ready, b + 1)
                        last = mm(o, wkk[:, :], cnT[:, b * J:(b + 1) * J])
                    elif t[0] == "V":
                        pe.wait_ge(cnT_ready, b + 1)
                        for i in range(JT):
                            k0 = b * J + i * P
                            last = mm(o[:, i * DH:(i + 1) * DH], cnT[:, k0:k0 + P], wv[:, :])
                    elif t[0] == "Q":
                        if b == 0:
                            pe.wait_ge(ld_q, 16)
                        pe.wait_ge(xnT_ready, b + 1)
                        last = mm(o[:, 0:N], wq[:, t[2] * P:(t[2] + 1) * P], xnT[:, b * N:(b + 1) * N])
                    elif t[0] == "M":
                        _, _, h, it = t
                        pe.wait_ge(ka_ready, b + 1)
                        pe.wait_ge(ql_ready, HP * b + h // 2 + 1)
                        last = mm(o, qa[:, b % 2, h, it * P:(it + 1) * P], ka[:, b * J:(b + 1) * J])
                    elif t[0] == "C":
                        half = t[2]
                        hs = slice(half * H // 2, (half + 1) * H // 2)
                        pe.wait_ge(c16_ready, 2 * b + half + 1)
                        o16 = o.bitcast(F16)
                        for it in range(IT):
                            last = nc.tensor.transpose(o16[0:H // 2, it * P:(it + 1) * P], c16[:, b, it, hs], ident16[:, :])
                    elif t[0] == "F":
                        _, ft, c, half = t
                        pe.wait_ge(ld_f, 16)
                        pe.wait_ge(xnT_ready, (c + 1) * CH // N)
                        f0 = (FF if half == 0 else 0) + ft * P
                        last = mm(o, wf1[:, f0:f0 + P], xnT[:, c * CH:(c + 1) * CH])
                    elif t[0] == "T":
                        _, _, it, half = t
                        pe.wait_ge(on_ready, HP * (b + 1))
                        for i in range(4):
                            hp = 4 * half + i
                            last = nc.tensor.transpose(
                                o[:, i * P:(i + 1) * P],
                                on[:, b % 2, it, 2 * hp:2 * hp + 2, :].rearrange("p h d -> p (h d)"), ident[:, :])
                    elif t[0] == "W":
                        tt = t[1]
                        pe.wait_ge(oT_ready, 2 * (tt + 1))
                        pe.wait_ge(ff_ready, FT * NCH)
                        pe.wait_ge(ld_o, 32)
                        cols = slice(tt * P, (tt + 1) * P)
                        for ft in range(FT):
                            mm(o[:, 0:DIM], ffT[:, ft, cols], wf2[:, ft, :], start=(ft == 0), stop=False)
                        for hp in range(HP):
                            last = mm(o[:, 0:DIM], oT[:, hp, tt // IT % 2, (tt % IT) * P:(tt % IT + 1) * P], wo[:, hp, :], start=False, stop=(hp == HP - 1))
                    last.then_inc(m_ready[n % MB], 1)

            pe.wait_ge(ld_m, 128)
            for n, t in enumerate(tail):
                k, o, c = n % 8, banks[n % 8], t[1]
                if n >= 8:
                    pe.wait_ge(*t_read(n - 8))
                elif k < MB:
                    pe.wait_ge(*m_read(max(i for i in range(len(tasks)) if i % MB == k)))
                elif k < MB + 4:
                    pe.wait_ge(ph_ready, CHUNKS)
                else:
                    pe.wait_ge(on_ready, UNITS)
                cols = slice(c * CH, (c + 1) * CH)
                if t[0] == "YT":
                    pe.wait_ge(y2_ready, c + 1)
                    for i in range(TPC):
                        last = nc.tensor.transpose(o[:, i * P:(i + 1) * P], yx[:, TPC * c + i, :], ident[:, :])
                elif t[0] == "L":
                    pe.wait_ge(y2T_ready, c + 1)
                    for i in range(TPC):
                        t0 = c * CH + i * P
                        last = mm(o[:, i * E:(i + 1) * E], y2T[:, t0:t0 + P], gw[:, :])
                elif t[0] in ("EG", "EU"):
                    p = t[2]
                    w = (wg if t[0] == "EG" else wu)[:, 2 * p:2 * p + 2, :].rearrange("h e i -> h (e i)") if p < EP \
                        else (wgs if t[0] == "EG" else wus)[:, :]
                    last = mm(o[0:(P if p < EP else I), :], w, y2T[:, cols])
                elif t[0] == "CWT":
                    pe.wait_ge(cw_ready, c + 1)
                    for i in range(TPC):
                        last = nc.tensor.transpose(o[0:E, i * P:(i + 1) * P], cw[:, i, :], ident[:, :])
                elif t[0] == "CB":
                    pe.wait_ge(cwT_ready, c + 1)
                    last = mm(o, esel[:, t[2], :, :].rearrange("k e i -> k (e i)"), cwT[:, c, :])
                else:
                    tt = t[1]
                    c = tt // TPC
                    pe.wait_ge(hE_ready, (2 * EP + 1) * (c + 1))
                    tc = slice(tt * P, (tt + 1) * P)
                    for p in range(EP):
                        mm(o[:, 0:DIM], hE(p)[:, tc], wd[:, p, :], start=(p == 0), stop=False)
                    last = mm(o[:, 0:DIM], hE(EP)[0:I, tc], wds[:, :], start=False)
                last.then_inc(t_ready[k], 1)

        @block.scalar
        def _(act):
            for item in order:
                if item[0] == "LN":
                    g = item[1]
                    lo, hi = (0, 1) if g == 0 else (1, B)
                    act.wait_ge(var_ready, 2 * g + 1)
                    nc.scalar.activation(rstd[:, XT + JT * lo:XT + JT * hi], rstd2[:, XT + JT * lo:XT + JT * hi],
                                         ACT.Sqrt)
                    nc.scalar.activation(rstd[:, IT * lo:IT * hi], rstd2[:, IT * lo:IT * hi], ACT.Sqrt).then_inc(std_ready, 1)
                    act.wait_ge(var_ready, 2 * g + 2)
                    nc.scalar.activation(rstd[:, IT * lo:IT * hi], rstd2[:, IT * lo:IT * hi], ACT.Sqrt).then_inc(std_ready, 1)
                    if g == 0:
                        act.wait_ge(ld_p, 96)
                    else:
                        nc.scalar.activation(tg[:, :], gates[:, :], ACT.Tanh).then_inc(tg_ready, 1)
                elif item[0] == "S":
                    _, u, jp = item
                    n = 2 * u + jp
                    act.wait_ge(s_ready, n + 1)
                    if n >= 4:
                        wait_split(act, n - 4)
                    if n >= PSLOTS:
                        act.wait_ge(o_ready, u - 2)
                    src = psS[:, 2 * (n % 2):2 * (n % 2) + 2, :]
                    nc.scalar.activation(p32[:, n % 4, :].rearrange("p (j c) -> p j c", j=2), src, ACT.Exp,
                                         scale=SM_SCALE).then_inc(p32_ready, 1)
                    nc.scalar.activation(ph[:, n % PSLOTS, :].rearrange("p (j c) -> p j c", j=2), src, ACT.Exp,
                                         scale=SM_SCALE).then_inc(ph_ready, 1)
                elif item[0] in ("PV", "O", "PL"):
                    pass
                else:
                    n = item[1]
                    t = tasks[n]
                    o, b = mbank(n), t[1]
                    ready = (m_ready[n % MB], n // MB + 1)
                    if t[0] == "CT":
                        act.wait_ge(*ready)
                        nc.scalar.activation(cnT[:, b * J:(b + 1) * J], o, ACT.Identity, bias=lnp[:, 3:4],
                                             scale=lnp[:, 2:3]).then_inc(cnT_ready, 1)
                    elif t[0] == "K":
                        act.wait_ge(*ready)
                        nc.scalar.activation(ka[:, b * J:(b + 1) * J], o, ACT.Copy).then_inc(ka_ready, 1)
                    elif t[0] == "V":
                        act.wait_ge(*ready)
                        nc.scalar.activation(vm[:, JT * b:JT * (b + 1), 0:DH],
                                             o[:, 0:JT * DH].rearrange("p (t d) -> p t d", d=DH),
                                             ACT.Copy).then_inc(vh_ready, 1)
                    elif t[0] == "F" and t[3] == 0:
                        act.wait_ge(*ready)
                        k = count("F", tasks, n) // 2
                        if k >= 2:
                            act.wait_ge(ff_ready, k - 1)
                        nc.scalar.activation(sg[:, k % 2, :], o, ACT.Silu).then_inc(sg_ready, 1)
                    elif t[0] == "T":
                        _, _, it, half = t
                        act.wait_ge(*ready)
                        if b >= 2:
                            act.wait_ge(x1_ready, IT * (b - 1))
                        nc.scalar.activation(oT[:, 4 * half:4 * half + 4, b % 2, it * P:(it + 1) * P],
                                             o.rearrange("p (h c) -> p h c", h=4),
                                             ACT.Copy).then_inc(oT_ready, 1)
            for c in range(NCH):
                act.wait_ge(var2_ready, c + 1)
                nc.scalar.activation(rstd[:, TPC * c:TPC * (c + 1)], rstd2[:, TPC * c:TPC * (c + 1)],
                                     ACT.Sqrt).then_inc(std2_ready, 1)
            for n, t in enumerate(tail):
                k, o, c = n % 8, banks[n % 8], t[1]
                if t[0] == "L":
                    act.wait_ge(t_ready[k], n // 8 + 1)
                    if c >= 1:
                        act.wait_ge(cw_ready, c)
                    nc.scalar.activation(es[:, :, :], o[:, 0:TPC * E].rearrange("p (t e) -> p t e", e=E), ACT.Exp,
                                         scale=-1.0).then_inc(es_ready, 1)
                elif t[0] == "EG":
                    act.wait_ge(t_ready[k], n // 8 + 1)
                    g = c * (EP + 1) + t[2]
                    if g >= 2:
                        act.wait_ge(hE_ready, hE_at[("EU", (g - 2) // (EP + 1), (g - 2) % (EP + 1))])
                    else:
                        act.wait_ge(ff_ready, FT * NCH)
                    rows = P if t[2] < EP else I
                    nc.scalar.activation(sg[0:rows, g % 2, :], o[0:rows, :], ACT.Silu).then_inc(sg_ready, 1)
                elif t[0] == "CWT":
                    act.wait_ge(t_ready[k], n // 8 + 1)
                    nc.scalar.activation(cwT[:, c, :], o[0:E, :], ACT.Copy).then_inc(cwT_ready, 1)

        @block.vector
        def _(dve):
            done = [0]

            def step(ins):
                done[0] += 1
                ins.then_inc(chain, 1)
                dve.wait_ge(chain, done[0])

            def statistics(tiles):
                for i, src in tiles:
                    last = nc.vector.bn_stats(stats[:, i, :], src)
                step(last)
                for i, _ in tiles:
                    last = nc.vector.bn_aggr(mv[:, i, :], stats[:, i, :])
                step(last)

            def layer_norms(g):
                lo, hi = (0, 1) if g == 0 else (1, B)
                for b in range(lo, hi):
                    dve.wait_ge(ld_c[b], 16)
                    dve.wait_ge(ld_x[b], 16)
                xt = list(range(IT * lo, IT * hi))
                ct = list(range(JT * lo, JT * hi))
                x_r, c_r = slice(IT * lo, IT * hi), slice(XT + JT * lo, XT + JT * hi)
                statistics([(i, xs[:, i, :]) for i in xt] + [(XT + i, cs[:, i, :]) for i in ct])
                nc.vector.tensor_scalar(rstd2[:, c_r], mv[:, c_r, 1], EPS, None, ALU.add)
                nc.vector.tensor_scalar(rstd2[:, x_r], mv[:, x_r, 1], EPS, None, ALU.add).then_inc(var_ready, 1)
                dve.wait_ge(std_ready, 2 * g + 1)
                rc = nc.vector.reciprocal(rstd2[:, c_r], rstd[:, c_r])
                if g == 1:
                    rc.then_inc(rs_ready, 1)
                step(nc.vector.reciprocal(rstd2[:, x_r], rstd[:, x_r]))
                for i in xt:
                    last = nc.vector.tensor_scalar(yx[:, i, :], xs[:, i, :], mv[:, i, 0:1], rstd2[:, i:i + 1],
                                                   ALU.subtract, ALU.mult)
                step(last)
                statistics([(i, yx[:, i, :]) for i in xt])
                nc.vector.tensor_scalar(rstd2[:, x_r], mv[:, x_r, 1], EPS, None, ALU.add).then_inc(var_ready, 1)
                if g == 0:
                    for i in ct:
                        last = nc.vector.tensor_scalar(cs[:, i, :], cs[:, i, :], mv[:, XT + i, 0:1],
                                                       rstd2[:, XT + i:XT + i + 1], ALU.subtract, ALU.mult)
                    last.then_inc(zc_ready, 1)
                dve.wait_ge(std_ready, 2 * g + 2)
                step(nc.vector.reciprocal(rstd2[:, x_r], rstd[:, x_r]))
                for i in xt:
                    last = nc.vector.tensor_scalar(yx[:, i, :], yx[:, i, :], mv[:, i, 0:1], rstd2[:, i:i + 1],
                                                   ALU.subtract, ALU.mult)
                last.then_inc(zx_ready, 1)
                if g == 0:
                    dve.wait_ge(ld_p, 96)

            for item in order:
                if item[0] == "LN":
                    layer_norms(item[1])
                elif item[0] == "PL":
                    n = item[1]
                    if n not in pooled:
                        if n >= PSLOTS:
                            dve.wait_ge(o_ready, n // 2 - 2)
                        dve.wait_ge(ph_ready, n + 1)
                        nc.vector.tensor_tensor(pl[:, n % PSLOTS, :], p32[:, n % 4, :], ph[:, n % PSLOTS, :],
                                                ALU.subtract).then_inc(pl_dve, 1)
                elif item[0] in ("PV", "S"):
                    pass
                elif item[0] == "O":
                    u = item[1]
                    b, hp = u // HP, u % HP
                    dve.wait_ge(o_ready, u + 1)
                    if b >= 2 and hp == 0:
                        dve.wait_ge(oT_ready, 4 * (b - 1))
                    o = psO[:, 0:2 * IT * OW].rearrange("p (h t w) -> p h t w", h=2, w=OW)
                    step(nc.vector.reciprocal(rden[:, u % 2, :, :], o[:, :, :, DH]))
                    nc.vector.tensor_tensor(
                        on[:, b % 2, :, 2 * hp:2 * hp + 2, :].rearrange("p t h d -> p h t d"), o[:, :, :, 0:DH],
                        rden[:, u % 2, :, :].unsqueeze(3).broadcast_to([P, 2, IT, DH]), ALU.mult).then_inc(on_ready, 1)
                else:
                    n = item[1]
                    t = tasks[n]
                    o, b = mbank(n), t[1]
                    ready = (m_ready[n % MB], n // MB + 1)
                    if t[0] == "XT":
                        dve.wait_ge(*ready)
                        nc.vector.tensor_scalar(xnT[:, b * N:(b + 1) * N], o[:, 0:N], lnp[:, 0:1], lnp[:, 1:2],
                                                ALU.mult, ALU.add).then_inc(xnT_ready, 1)
                    elif t[0] == "K":
                        dve.wait_ge(ka_ready, b + 1)
                        cols = slice(b * J, (b + 1) * J)
                        nc.vector.tensor_tensor(kb[0:DH, cols], o[0:DH, :], ka[0:DH, cols],
                                                ALU.subtract).then_inc(kb_ready, 1)
                    elif t[0] == "V":
                        dve.wait_ge(vh_ready, b + 1)
                        nc.vector.tensor_tensor(vm[:, JT * b:JT * (b + 1), DH + 1:VW],
                                                o[:, 0:JT * DH].rearrange("p (t d) -> p t d", d=DH),
                                                vm[:, JT * b:JT * (b + 1), 0:DH],
                                                ALU.subtract).then_inc(vl_ready, 1)
                    elif t[0] == "Q":
                        p, s = t[2], b % 2
                        if b >= 2 and p % HALF == 0:
                            dve.wait_ge(qb_ready, 16 * (2 * (b - 2) + p // HALF + 1))
                        dve.wait_ge(*ready)
                        nc.vector.tensor_copy(qa[0:DH, s, 2 * p, :], o[0:DH, 0:N])
                        step(nc.vector.tensor_copy(qa[0:DH, s, 2 * p + 1, :], o[DH:P, 0:N]))
                        nc.vector.tensor_tensor(qa[DH:P, s, 2 * p, :], o[0:DH, 0:N], qa[0:DH, s, 2 * p, :], ALU.subtract)
                        nc.vector.tensor_tensor(qa[DH:P, s, 2 * p + 1, :], o[DH:P, 0:N], qa[0:DH, s, 2 * p + 1, :],
                                                ALU.subtract).then_inc(ql_ready, 1)
                    elif t[0] == "M":
                        _, _, h, it = t
                        dve.wait_ge(*ready)
                        nc.vector.tensor_reduce(mx[:, b, it, h:h + 1], o, AX_X,
                                                ALU.max).then_inc(mx_ready, 1)
                    elif t[0] == "C":
                        hs = slice(t[2] * H // 2, (t[2] + 1) * H // 2)
                        dve.wait_ge(mx_ready, H * IT // 2 * (2 * b + t[2] + 1))
                        nc.vector.tensor_scalar(c16[:, b, :, hs], mx[:, b, :, hs], -1.0 / SHIFT, None,
                                                ALU.mult).then_inc(c16_ready, 1)
                        dve.wait_ge(*ready)
                        nc.vector.tensor_copy(cT[:, b, t[2], :], o.bitcast(F16)[0:H // 2, 0:N]).then_inc(cT_ready, 1)
                    elif t[0] == "F" and t[3] == 1:
                        _, ft, c, _ = t
                        k = count("F", tasks, n) // 2
                        dve.wait_ge(sg_ready, k + 1)
                        dve.wait_ge(*ready)
                        nc.vector.tensor_tensor(ffT[:, ft, c * CH:(c + 1) * CH], o, sg[:, k % 2, :],
                                                ALU.mult).then_inc(ff_ready, 1)
                    elif t[0] == "W":
                        tt = t[1]
                        dve.wait_ge(*ready)
                        dve.wait_ge(tg_ready, 1)
                        nc.vector.scalar_tensor_tensor(x1[:, tt, :], o[:, 0:DIM], tg[:, 0:1], xs[:, tt, :],
                                                       ALU.mult, ALU.add).then_inc(x1_ready, 1)

            for c in range(NCH):
                ts = list(range(TPC * c, TPC * (c + 1)))
                r = slice(TPC * c, TPC * (c + 1))
                dve.wait_ge(x1_ready, TPC * (c + 1))
                statistics([(i, x1[:, i, :]) for i in ts])
                nc.vector.tensor_scalar(rstd2[:, r], mv[:, r, 1], EPS, None, ALU.add).then_inc(var2_ready, 1)
            for c in range(NCH):
                ts = list(range(TPC * c, TPC * (c + 1)))
                r = slice(TPC * c, TPC * (c + 1))
                dve.wait_ge(std2_ready, c + 1)
                step(nc.vector.reciprocal(rstd2[:, r], rstd[:, r]))
                for i in ts:
                    last = nc.vector.tensor_scalar(yx[:, i, :], x1[:, i, :], mv[:, i, 0:1], rstd2[:, i:i + 1],
                                                   ALU.subtract, ALU.mult)
                last.then_inc(y2_ready, 1)

            def route(c):
                pair = [P, TPC, E, E]
                gpair = [P, TPC, NG, NG]
                dve.wait_ge(es_ready, c + 1)
                step(nc.vector.tensor_scalar(es[:, :, :], es[:, :, :], 1.0, None, ALU.add))
                step(nc.vector.reciprocal(sc[:, :, :], es[:, :, :]))
                step(nc.vector.tensor_tensor(scc[:, :, :], sc[:, :, :],
                                             cb[:, :].unsqueeze(1).broadcast_to([P, TPC, E]), ALU.add))
                step(nc.vector.tensor_reduce(grp[:, :, :], scc[:, :, :].rearrange("p t (g m) -> p t g m", m=EPG),
                                             AX_X, ALU.add))
                other, own = grp[:, :, :].unsqueeze(2).broadcast_to(gpair), grp[:, :, :].unsqueeze(3).broadcast_to(gpair)
                a, bb = cmpA[:, :, 0:NG, 0:NG], cmpB[:, :, 0:NG, 0:NG]
                nc.vector.tensor_tensor(a, other, own, ALU.is_gt)
                step(nc.vector.tensor_tensor(bb, other, own, ALU.is_equal))
                step(nc.vector.tensor_tensor(bb, bb, lower[:, 0:NG, 0:NG].unsqueeze(1).broadcast_to(gpair), ALU.mult))
                step(nc.vector.tensor_tensor(a, a, bb, ALU.add))
                step(nc.vector.tensor_reduce(grank[:, :, :], a, AX_X, ALU.add))
                step(nc.vector.tensor_scalar(gsel[:, :, :], grank[:, :, :], float(TKG), None, ALU.is_lt))
                step(nc.vector.tensor_tensor(choice[:, :, :].rearrange("p t (g m) -> p t g m", m=EPG),
                                             scc[:, :, :].rearrange("p t (g m) -> p t g m", m=EPG),
                                             gsel[:, :, :].unsqueeze(3).broadcast_to([P, TPC, NG, EPG]), ALU.mult))
                other, own = choice[:, :, :].unsqueeze(2).broadcast_to(pair), choice[:, :, :].unsqueeze(3).broadcast_to(pair)
                nc.vector.tensor_tensor(cmpA[:, :, :, :], other, own, ALU.is_gt)
                step(nc.vector.tensor_tensor(cmpB[:, :, :, :], other, own, ALU.is_equal))
                step(nc.vector.tensor_tensor(cmpB[:, :, :, :], cmpB[:, :, :, :],
                                             lower[:, :, :].unsqueeze(1).broadcast_to(pair), ALU.mult))
                step(nc.vector.tensor_tensor(cmpA[:, :, :, :], cmpA[:, :, :, :], cmpB[:, :, :, :], ALU.add))
                step(nc.vector.tensor_reduce(rank[:, :, :], cmpA[:, :, :, :], AX_X, ALU.add))
                step(nc.vector.tensor_scalar(rank[:, :, :], rank[:, :, :], float(TOPK), None, ALU.is_lt))
                step(nc.vector.tensor_tensor(sc[:, :, :], sc[:, :, :], rank[:, :, :], ALU.mult))
                step(nc.vector.tensor_reduce(wsum[:, :], sc[:, :, :], AX_X, ALU.add))
                step(nc.vector.tensor_scalar(wsum[:, :], wsum[:, :], 1e-20, None, ALU.add))
                step(nc.vector.reciprocal(wsum[:, :], wsum[:, :]))
                step(nc.vector.tensor_scalar(wsum[:, :], wsum[:, :], ROUTE_SCALE, None, ALU.mult))
                if c >= 1:
                    dve.wait_ge(cwT_ready, c)
                nc.vector.tensor_tensor(cw[:, :, :], sc[:, :, :], wsum[:, :].unsqueeze(2).broadcast_to([P, TPC, E]),
                                        ALU.mult).then_inc(cw_ready, 1)

            for n, t in enumerate(tail):
                k, o, c = n % 8, banks[n % 8], t[1]
                ready = (t_ready[k], n // 8 + 1)
                cols = slice(c * CH, (c + 1) * CH)
                if t[0] == "YT":
                    dve.wait_ge(*ready)
                    nc.vector.tensor_copy(y2T[:, cols], o).then_inc(y2T_ready, 1)
                elif t[0] == "L":
                    if c == 1:
                        continue
                    route(c)
                elif t[0] == "EU":
                    g = c * (EP + 1) + t[2]
                    rows = P if t[2] < EP else I
                    dve.wait_ge(sg_ready, FT * NCH + g + 1)
                    dve.wait_ge(*ready)
                    last = nc.vector.tensor_tensor(hE(t[2])[0:rows, cols], o[0:rows, :], sg[0:rows, g % 2, :], ALU.mult)
                    last.then_inc(hE_ready, 1)
                    if c == 0 and t[2] == EP:
                        route(1)
                elif t[0] == "CB":
                    dve.wait_ge(*ready)
                    dve.wait_ge(hE_ready, hE_at[("EU", c, t[2])])
                    last = nc.vector.tensor_tensor(hE(t[2])[:, cols], hE(t[2])[:, cols], o, ALU.mult)
                    last.then_inc(hE_ready, 1)
                elif t[0] == "D":
                    dve.wait_ge(*ready)
                    nc.vector.scalar_tensor_tensor(outt[:, t[1], :], o[:, 0:DIM], tg[:, 1:2], x1[:, t[1], :],
                                                   ALU.mult, ALU.add).then_inc(out_ready, 1)


_INS = ["x", "ctx_1024", "g_xattn", "g_ffn", "L0_xattn_ln_g", "L0_xattn_ln_b", "L0_xattn_cln_g", "L0_xattn_cln_b",
        "L0_xattn_Wq", "L0_xattn_Wkv", "L0_xattn_Wo", "L0_xattn_Wff1", "L0_xattn_Wff2", "L0_ffn_gate_w",
        "L0_ffn_correction_bias", "L0_ffn_Wg", "L0_ffn_Wu", "L0_ffn_Wd", "L0_ffn_Wg_s", "L0_ffn_Wu_s", "L0_ffn_Wd_s"]


def kernel(**inputs):
    import numpy as _np
    import concourse.bacc as _bacc
    from concourse import mybir as _mybir
    from concourse.bass_utils import run_bass_kernel_spmd as _run

    nc = _bacc.Bacc("TRN2", target_bir_lowering=False, num_devices=1)
    arrays, args = {}, []
    for name in _INS:
        a = _np.asarray(inputs[name])
        if name == "L0_ffn_gate_w":
            a = a.T
        a = _np.ascontiguousarray(a)
        arrays[f"in_{name}"] = a
        args.append(nc.dram_tensor(f"in_{name}", a.shape, _mybir.dt.from_np(a.dtype), kind="ExternalInput").ap())
    shape = _np.asarray(inputs["x"]).shape
    args.append(nc.dram_tensor("out_x", shape, _mybir.dt.float32, kind="ExternalOutput").ap())
    flamingo_gated_moe(nc, *args)
    r = _run(nc, [arrays], core_ids=[0])
    return r.results[0]["out_x"]
```

```python
from contextlib import ExitStack

import concourse.bass as bass
from concourse import mybir

P = 128
F32 = mybir.dt.float32
F16 = mybir.dt.float16
ALU = mybir.AluOpType
ACT = mybir.ActivationFunctionType
AX_X = mybir.AxisListType.X


def flamingo_gated_moe(nc, x, ctx_in, g_xattn, g_ffn, ln_g, ln_b, cln_g, cln_b, Wq, Wkv, Wo, Wff1, Wff2,
                       gate_wT, cbias, Wg, Wu, Wd, Wg_s, Wu_s, Wd_s, out):
    B, N, DIM = x.shape
    J = ctx_in.shape[1]
    INNER = Wq.shape[1]
    DH = Wkv.shape[1] // 2
    H = INNER // DH
    FF = Wff2.shape[0]
    E, _, I = Wg.shape
    NG, TKG, TOPK, ROUTE_SCALE = 4, 2, 4, 2.5
    EPG = E // NG
    assert DIM == P and 2 * DH == P and 2 * I == P and J % P == 0 and N % P == 0
    EPS = 1e-5
    SM_SCALE = DH ** -0.5
    SHIFT = 16.0
    TOK = B * N
    XT = TOK // P
    CT = B * J // P
    IT = N // P
    JT = J // P
    HP = H // 2
    FT = FF // P
    EP = E // 2
    CH = 512
    VW = 2 * DH + 1
    MB = 3
    OW = DH + 1
    UNITS = B * HP
    CHUNKS = 2 * UNITS
    PSLOTS = 6
    LAG = 2
    LEAD = 3
    QLEAD = LEAD + 2

    with ExitStack() as stack:
        def sb(name, shape, dt=F32):
            return stack.enter_context(nc.sbuf_tensor(name, shape, dt))

        def sem(name):
            return stack.enter_context(nc.semaphore(name))

        psM = stack.enter_context(nc.psum_tensor("psM", [P, MB, 512], F32))
        psS = stack.enter_context(nc.psum_tensor("psS", [P, 4, 512], F32))
        psO = stack.enter_context(nc.psum_tensor("psO", [P, 512], F32))
        banks = [psM[:, i, :] for i in range(MB)] + [psS[:, i, :] for i in range(4)] + [psO[:, :]]

        xs = sb("xs", [P, XT, DIM])
        yx = sb("yx", [P, XT, DIM])
        cs = sb("cs", [P, CT, DIM])
        stats = sb("stats", [P, XT + CT, 6])
        mv = sb("mv", [P, XT + CT, 2])
        vare = sb("vare", [P, XT + CT])
        std = sb("std", [P, XT + CT])
        rstd = sb("rstd", [P, XT + CT])
        xnT = sb("xnT", [P, 2, TOK], F16)
        xn32 = sb("xn32", [P, N])
        cnT = sb("cnT", [P, 2 * J])
        wq = sb("wq", [P, 2, INNER], F16)
        wf1 = sb("wf1", [P, 2, 2 * FF], F16)
        wo = sb("wo", [P, 2, HP * DIM], F16)
        wgu = sb("wgu", [P, 2, 2 * E * I], F16)
        wsm = sb("wsm", [P, 2, 2 * I + E], F16)
        wkk = sb("wkk", [P, 2 * DH])
        wv = sb("wv", [P, DH])
        wf2 = sb("wf2", [P, FT, DIM])
        wd = sb("wd", [P, EP, DIM])
        wds = sb("wds", [I, DIM])
        wsm32 = sb("wsm32", [P, 2 * I + E])
        cb = sb("cb", [P, E])
        lnp = sb("lnp", [P, 4])
        gates = sb("gates", [P, 2])
        tg = sb("tg", [P, 2])
        ident = sb("ident", [P, P])
        ident16 = sb("ident16", [P, P], F16)
        lower = sb("lower", [P, E, E])
        esel = sb("esel", [2 * E, EP, 2, I], F16)
        qa = sb("qa", [P, 2, H, N], F16)
        qb = sb("qb", [DH + 1, 2, H, N], F16)
        ka = sb("ka", [P, B * J], F16)
        kb = sb("kb", [DH + 1, B * J], F16)
        vm = sb("vm", [P, CT, VW], F16)
        mx = sb("mx", [P, B, IT, H])
        c16 = sb("c16", [P, B, IT, H], F16)
        cT = sb("cT", [2, 2, HP, N], F16)
        p32 = sb("p32", [P, 4, 2 * CH])
        ph = sb("ph", [P, PSLOTS, 2 * CH], F16)
        pl = sb("pl", [P, PSLOTS, 2 * CH], F16)
        rden = sb("rden", [P, 2, 2, IT])
        on32 = sb("on32", [P, 2, IT, 2, DH])
        on = sb("on", [P, 2, 2, IT, H, DH], F16)
        oT = sb("oT", [P, 2, HP, 2, N], F16)
        act_g = sb("act_g", [P, 2, N])
        act_u = sb("act_u", [P, 2, N])
        gu = sb("gu", [P, 2, 2 * N])
        ffT = sb("ffT", [P, FT, TOK])
        hS = sb("hS", [I, TOK])
        cmpA = sb("cmpA", [P, IT, E, E])
        cmpB = sb("cmpB", [P, IT, E, E])
        es = sb("es", [P, IT, E])
        sc = sb("sc", [P, IT, E])
        scc = sb("scc", [P, IT, E])
        grp = sb("grp", [P, IT, NG])
        gsel = sb("gsel", [P, IT, NG])
        choice = sb("choice", [P, IT, E])
        rank = sb("rank", [P, IT, E])
        grank = sb("grank", [P, IT, NG])
        wsum = sb("wsum", [P, IT])
        cw = sb("cw", [P, IT, E])
        cw16 = sb("cw16", [P, IT, 2 * E], F16)
        cwT = sb("cwT", [2 * E, 2, N], F16)
        wstage = p32
        x1 = xs
        y2T = xnT
        outt = cs

        ld_x = [sem(f"ld_x{b}") for b in range(B)]
        ld_c = [sem(f"ld_c{b}") for b in range(B)]
        ld_p = sem("ld_p")
        ld_k, ld_q = sem("ld_k"), sem("ld_q")
        ld_f, ld_o, ld_m, ld_e, ld_s = sem("ld_f"), sem("ld_o"), sem("ld_m"), sem("ld_e"), sem("ld_s")
        wh_ready, wl_ready = sem("wh_ready"), sem("wl_ready")
        consts = sem("consts")
        chain = sem("chain")
        tg_ready = sem("tg_ready")
        idents = sem("idents")
        var_ready = [sem(f"var{b}_ready") for b in range(B)]
        std_ready = [sem(f"std{b}_ready") for b in range(B)]
        rs_ready = [sem(f"rs{b}_ready") for b in range(B)]
        zx_ready = [sem(f"zx{b}_ready") for b in range(B)]
        zc_ready = [sem(f"zc{b}_ready") for b in range(B)]
        ready = [sem(f"bank{k}_ready") for k in range(8)]
        xnT_ready, cnT_ready = sem("xnT_ready"), sem("cnT_ready")
        ka_ready, kb_ready = sem("ka_ready"), sem("kb_ready")
        vh_ready, vl_ready = sem("vh_ready"), sem("vl_ready")
        qh_ready, ql_ready = sem("qh_ready"), sem("ql_ready")
        qb_ready = [[sem(f"qb{s}_{g}_ready") for g in range(HP)] for s in range(2)]
        crow_ready = [[sem(f"crow{s}_{g}_ready") for g in range(HP)] for s in range(2)]
        mx_ready = sem("mx_ready")
        c16_ready, cT_ready = sem("c16_ready"), sem("cT_ready")
        s_ready = sem("s_ready")
        ph_ready = sem("ph_ready")
        p32_ready = sem("p32_ready")
        pl_dve, pl_pool = sem("pl_dve"), sem("pl_pool")
        o_ready, on_ready = sem("o_ready"), sem("on_ready")
        onh_ready, onl_ready = sem("onh_ready"), sem("onl_ready")
        oT_ready = sem("oT_ready")
        oT_dve = sem("oT_dve")
        th_ready = sem("th_ready")
        gated = sem("gated")
        gated_pool = sem("gated_pool")
        gu_ready = sem("gu_ready")
        pool_chain = sem("pool_chain")
        scaled = sem("scaled")
        xa_ready = sem("xa_ready")
        x1_ready = sem("x1_ready")
        y_var_ready, y_std_ready = sem("y_var_ready"), sem("y_std_ready")
        y2_ready, y2T_ready = sem("y2_ready"), sem("y2T_ready")
        es_ready, cw_ready, cwT_ready = sem("es_ready"), sem("cw_ready"), sem("cwT_ready")
        out_ready, stored = sem("out_ready"), sem("stored")

        tasks, bank_of, order = [], [], []
        phase = []

        def task(*t):
            order.append(("task", len(tasks)))
            bank_of.append(len(tasks) % (MB if now == 1 else 8))
            tasks.append(t)
            phase.append(now)

        def maxima(u):
            b, hp = u // HP, u % HP
            return [("M", b, 2 * hp + h, it) for h in range(2) for it in range(IT)] if u < UNITS else []

        def emit(*ts):
            for t in ts:
                if t[0] in ("STAT", "ROOT", "NORM", "NEG", "SPLIT", "ST", "SQ", "WARM", "RTA", "RTB", "RTC"):
                    order.append(t)
                else:
                    task(*t)

        now = 0
        emit(("STAT", 0), ("ROOT", 0), ("NORM", 0), ("SPLIT", 0), ("XT", 0), ("CT", 0), ("STAT", 1), ("STAT", 2),
             ("K", 0), ("Q", 0, 0), ("ROOT", 1), *[("NORM", 1, i) for i in range(IT + JT)], ("ROOT", 2), ("SPLIT", 1),
             *maxima(0), ("NEG", 0, 0), ("Q", 0, 1), ("C", 0, 0), ("STAT", 3), ("SPLIT", 2), *maxima(1),
             ("NEG", 0, 1), ("SPLIT", 3), ("ROOT", 3), ("Q", 0, 2), ("V", 0), ("Q", 0, 3), ("C", 0, 1))
        now = 1
        side = [[] for _ in range(UNITS + LAG)]

        def at(u, *ts):
            side[u].extend(ts)

        at(0, ("XT", 1), ("CT", 1), ("K", 1))
        at(2, ("V", 1))
        for b, k, v in ((2, 9, 9), (3, 16, 19)):
            at(k, ("K", b))
            at(v, ("V", b))
        for b, tiles, xt, ct in ((2, (1, 2, 3, 4, 5, 6), 4, 7),
                                 (3, (7, 8, 9, 10, 11, 12), 10, 14)):
            for i, u in enumerate(tiles):
                at(u, ("NORM", b, i))
            at(xt, ("XT", b))
            at(ct, ("CT", b))
        for i, u in enumerate((1, 4, 3, 10, 10, 9, 11, 12, 12, 14, 17, 23, 22, 21, 29, 30)):
            at(u, ("F", i // FT, i % FT))
        first_half = (6, 14, 23, 30)
        for b, units in enumerate((
                (10, 11, 12, 12, 14, 15, 16, 18, 18, 18, 18, 19, 19, 20, 20, 21, 21, 22, 22, 23, 25),
                (18, 18, 19, 20, 21, 22, 23, 24, 24, 25, 25, 26, 26, 27, 27, 28, 28, 29, 29, 31, 32),
                (26, 26, 27, 27, 28, 29, 30, 31, 31, 31, 32, 32, 32, 33, 33, 33, 33, 33, 33))):
            steps = [("T", b, 0, 1), ("T", b, 1, 1), ("W", IT * b), ("W", IT * b + 1), ("ST", b), ("SQ", b), ("YT", b),
                     ("L", b)]
            if b < B - 2:
                steps += [("E", b, 0), ("RTA", b), ("E", b, 1), ("RTB", b), ("E", b, 2), ("RTC", b), ("E", b, 3),
                          ("CWT", b), ("E", b, 4)]
            else:
                steps += [("RTA", b), ("E", b, 0), ("RTB", b), ("E", b, 1), ("E", b, 2), ("RTC", b), ("E", b, 3),
                          ("E", b, 4), ("CWT", b)]
            steps += [("CB", b, 0), ("CB", b, 1), ("D", IT * b), ("D", IT * b + 1)]
            at(first_half[b], ("T", b, 0, 0), ("T", b, 1, 0))
            for t, u in zip(steps, units):
                at(u, t)
        at(first_half[B - 1], ("T", B - 1, 0, 0), ("T", B - 1, 1, 0))
        at(31, ("WA", IT * (B - 1)))
        at(32, ("WA", IT * (B - 1) + 1))
        for u in range(UNITS + LAG):
            ms = maxima(u + LEAD)
            if u < UNITS:
                order.append(("S", u, 0))
            if u == 0:
                emit(*maxima(LEAD - 1), ("NEG", 0, LEAD - 1), ("Q", 0, QLEAD - 1))
            if u + QLEAD >= UNITS and u + 2 < UNITS:
                emit(("C", (u + 2) // HP, (u + 2) % HP))
            emit(*ms[:2])
            if 1 <= u <= UNITS:
                order.append(("PL", 2 * u - 1))
            if u >= UNITS:
                emit(*side[u])
            if u >= LAG:
                order.append(("PV", u - LAG, 0))
            if u < UNITS:
                emit(*side[u])
                order.append(("S", u, 1))
            emit(*ms[2:])
            if ms:
                emit(("NEG", (u + LEAD) // HP, (u + LEAD) % HP))
            if u >= LAG:
                order.append(("PV", u - LAG, 1))
                order.append(("O", u - LAG))
            if u + QLEAD < UNITS:
                emit(("Q", (u + QLEAD) // HP, (u + QLEAD) % HP, u + 2))

        now = 2
        b, c = B - 1, B - 2
        emit(("T", b, 0, 1), ("T", b, 1, 1), ("WARM",), ("D", IT * c), ("WB", IT * b), ("WB", IT * b + 1), ("ST", b),
             ("D", IT * c + 1), ("SQ", b), ("YT", b), ("L", b), ("RTA", b), ("E", b, 0), ("RTB", b), ("E", b, 1), ("RTC", b),
             ("E", b, 2), ("E", b, 3), ("E", b, 4), ("CWT", b), ("CB", b, 0), ("CB", b, 1), ("D", IT * b), ("D", IT * b + 1))

        def before(n, kinds):
            return sum(1 for t in tasks[:n] if t[0] in kinds)

        def stands(n):
            return ready[bank_of[n]], sum(1 for m in range(n + 1) if bank_of[m] == bank_of[n])

        def read_out(n):
            t = tasks[n]
            same = before(n, (t[0],)) + 1
            if t[0] in ("F", "E"):
                return (gu_ready, pooled_gates(n)) if by_pool(t) else gate(n)
            if by_dve(t):
                return oT_dve, 1
            if t[0] == "C":
                return cT_ready, unit_of(t) + 1
            if t[0] in ("W", "WB"):
                return x1_ready, before(n, ("W", "WB")) + 1
            return {"XT": xnT_ready, "CT": cnT_ready, "K": kb_ready, "V": vl_ready, "Q": ql_ready, "M": mx_ready,
                    "T": oT_ready, "WA": xa_ready, "YT": y2T_ready, "L": es_ready, "CB": scaled, "CWT": cwT_ready,
                    "D": out_ready}[t[0]], same

        def unit_of(t):
            return t[1] * HP + t[2]

        def nth(n):
            return before(n, ("F", "E")) + 1

        def by_dve(t):
            return t == ("T", B - 1, IT - 1, 1)

        def by_pool(t):
            return t[0] == "E" and t[1] < 2 or t[0] == "F" and t[1] >= 2

        def pooled_gates(n):
            return sum(1 for t in tasks[:n + 1] if t[0] in ("F", "E") and by_pool(t))

        def gate(n):
            return (gated_pool, pooled_gates(n)) if by_pool(tasks[n]) else (gated, nth(n) - pooled_gates(n))

        def gated_by(*t):
            return gate(tasks.index(t))

        def nth_gate(g):
            return [n for n, t in enumerate(tasks) if t[0] in ("F", "E")][g - 1]

        def scaled_by(c, p):
            return before(tasks.index(("CB", c, p // 2)), ("CB",)) + 1

        pooled = {n for n in range(CHUNKS) if n % 8 != 3}

        def wait_split(eng, n):
            if n in pooled:
                eng.wait_ge(pl_pool, sum(1 for m in pooled if m <= n))
            else:
                eng.wait_ge(pl_dve, n + 1 - sum(1 for m in pooled if m <= n))

        splits = [(wstage[:, 0, :], wq, ld_q, 16), (wstage[:, 1, :], wf1, ld_f, 16),
                  (wstage[:, 2, :], wgu, ld_e, 32), (wstage[:, 3, :], wo, ld_o, 16)]

        block = stack.enter_context(nc.Block())

        c_t = ctx_in.rearrange("b (t p) d -> p (b t) d", p=P)

        @block.sync
        def _(sp):
            x_t = x.rearrange("b (t p) d -> p (b t) d", p=P)
            for b in range(B):
                sp.dma_start(xs[:, IT * b:IT * (b + 1), :], x_t[:, IT * b:IT * (b + 1), :]).then_inc(ld_x[b], 16)
                if b > 0:
                    sp.dma_start(cs[:, JT * b:JT * (b + 1), :], c_t[:, JT * b:JT * (b + 1), :]).then_inc(ld_c[b], 16)
                if b == 0:
                    sp.dma_start(wkk[:, 0:DH], Wkv[:, 0:DH]).then_inc(ld_k, 16)
                    sp.dma_start(wkk[:, DH:2 * DH], Wkv[:, 0:DH]).then_inc(ld_k, 16)
                    sp.dma_start(wv[:, :], Wkv[:, DH:2 * DH]).then_inc(ld_k, 16)
                    sp.dma_start(wstage[:, 0, :], Wq).then_inc(ld_q, 16)
                if b == 1:
                    sp.dma_start(wstage[:, 1, :], Wff1).then_inc(ld_f, 16)
                    sp.dma_start(wstage[:, 2, 0:E * I].rearrange("p (e i) -> p e i", e=E),
                                 Wg.rearrange("e h i -> h e i")).then_inc(ld_e, 16)
                    sp.dma_start(wstage[:, 2, E * I:2 * E * I].rearrange("p (e i) -> p e i", e=E),
                                 Wu.rearrange("e h i -> h e i")).then_inc(ld_e, 16)
            sp.dma_start(wstage[:, 3, :].rearrange("p (h d) -> p h d", h=HP),
                         Wo.rearrange("(p r) d -> r p d", r=P)).then_inc(ld_o, 16)
            sp.dma_start(wsm32[:, 0:I], Wg_s).then_inc(ld_s, 16)
            sp.dma_start(wsm32[:, I:2 * I], Wu_s).then_inc(ld_s, 16)
            sp.dma_start(wsm32[:, 2 * I:2 * I + E], gate_wT).then_inc(ld_s, 16)
            for b in range(B):
                for g in range(HP):
                    hs = slice(2 * g, 2 * g + 2)
                    sp.wait_ge(ql_ready, HP * b + g + 1)
                    if b >= 2:
                        sp.wait_ge(s_ready, 2 * (HP * (b - 2) + g + 1))
                    sp.dma_start(qb[0:DH, b % 2, hs, :], qa[0:DH, b % 2, hs, :]).then_inc(qb_ready[b % 2][g], 16)
                    sp.wait_ge(cT_ready, HP * b + g + 1)
                    sp.dma_start(qb[DH:DH + 1, b % 2, hs, :], cT[:, b % 2, g, :]).then_inc(crow_ready[b % 2][g], 16)
                    if b == 0 and g == 1:
                        sp.dma_start(wf2[:, :, :], Wff2.rearrange("(p r) d -> r p d", r=P)).then_inc(ld_m, 16)
                        sp.dma_start(wd[:, :, :], Wd.rearrange("(p e) i d -> (e i) p d", e=2)).then_inc(ld_m, 16)
                        sp.dma_start(wds[:, :], Wd_s).then_inc(ld_m, 16)
                        sp.dma_start(cb[:, :], cbias.rearrange("(a e) -> a e", a=1).broadcast_to([P, E])).then_inc(ld_m, 16)
            o_t = out.rearrange("b (t p) d -> p (b t) d", p=P)
            for t in range(XT):
                sp.wait_ge(out_ready, t + 1)
                sp.dma_start(o_t[:, t, :], outt[:, t, :]).then_inc(stored, 16)
            sp.wait_ge(stored, 16 * XT)

        @block.gpsimd
        def _(pool):
            nc.gpsimd.memset(ident[:, :], 0.0).then_inc(idents, 1)
            nc.gpsimd.memset(ident16[:, :], 0.0).then_inc(idents, 1)
            pool.wait_ge(idents, 2)
            for m in (ident, ident16):
                nc.gpsimd.affine_select(out=m[:, :], in_=m[:, :], compare_op=ALU.not_equal, fill=1.0, base=0,
                                        pattern=[[-1, P]], channel_multiplier=1).then_inc(idents, 1)
            nc.gpsimd.memset(lower[:, :, :], 0.0).then_inc(consts, 1)
            nc.gpsimd.memset(esel[:, :, :, :], 0.0).then_inc(consts, 1)
            nc.gpsimd.memset(vm[:, :, DH:DH + 1], 1.0).then_inc(consts, 1)
            pool.wait_ge(idents, 4)
            pool.wait_ge(consts, 3)
            nc.gpsimd.memset(kb[DH:DH + 1, :], SHIFT).then_inc(consts, 1)
            pool.wait_ge(consts, 4)
            nc.gpsimd.affine_select(out=lower[:, :, :], in_=lower[:, :, :], compare_op=ALU.is_ge, fill=1.0, base=0,
                                    pattern=[[-1, E], [1, E]], channel_multiplier=0).then_inc(consts, 1)
            nc.gpsimd.affine_select(out=esel[:, :, :, :], in_=esel[:, :, :, :], compare_op=ALU.not_equal, fill=1.0,
                                    base=0, pattern=[[-2, EP], [-1, 2], [0, I]], channel_multiplier=1).then_inc(consts, 1)
            pool.wait_ge(consts, 6)
            nc.gpsimd.affine_select(out=esel[:, :, :, :], in_=esel[:, :, :, :], compare_op=ALU.not_equal, fill=1.0,
                                    base=-E, pattern=[[-2, EP], [-1, 2], [0, I]], channel_multiplier=1).then_inc(consts, 1)
            for item in order:
                if item[0] == "NORM" and item[1] > 0:
                    _, b, k = item
                    pool.wait_ge(rs_ready[b], 1)
                    if k < IT:
                        i = IT * b + k
                        last = nc.gpsimd.tensor_scalar(yx[:, i, :], xs[:, i, :], mv[:, i, 0:1], rstd[:, i:i + 1],
                                                       ALU.subtract, ALU.mult)
                        if k == IT - 1:
                            last.then_inc(zx_ready[b], 1)
                    else:
                        i = JT * b + k - IT
                        last = nc.gpsimd.tensor_scalar(cs[:, i, :], cs[:, i, :], mv[:, XT + i, 0:1],
                                                       rstd[:, XT + i:XT + i + 1], ALU.subtract, ALU.mult)
                        if k == IT + JT - 1:
                            last.then_inc(zc_ready[b], 1)
                elif item[0] == "SPLIT":
                    k = item[1]
                    src, w, _, _ = splits[k]
                    pool.wait_ge(wh_ready, k + 1)
                    nc.gpsimd.tensor_tensor(w[:, 1, :], src, w[:, 0, :], ALU.subtract).then_inc(wl_ready, 1)
                    if k == len(splits) - 1:
                        pool.wait_ge(wh_ready, k + 2)
                        nc.gpsimd.tensor_tensor(wsm[:, 1, :], wsm32[:, :], wsm[:, 0, :], ALU.subtract).then_inc(wl_ready, 1)
                elif item[0] == "O":
                    u = item[1]
                    b, hp = u // HP, u % HP
                    pool.wait_ge(onh_ready, u + 1)
                    nc.gpsimd.tensor_tensor(on[:, 1, b % 2, :, 2 * hp:2 * hp + 2, :], on32[:, u % 2, :, :, :],
                                            on[:, 0, b % 2, :, 2 * hp:2 * hp + 2, :], ALU.subtract).then_inc(onl_ready, 1)
                elif item[0] == "S":
                    n = 2 * item[1] + item[2]
                    if n in pooled:
                        if n >= PSLOTS:
                            pool.wait_ge(o_ready, item[1] - 2)
                        pool.wait_ge(ph_ready, n + 1)
                        nc.gpsimd.tensor_tensor(pl[:, n % PSLOTS, :], p32[:, n % 4, :], ph[:, n % PSLOTS, :],
                                                ALU.subtract).then_inc(pl_pool, 1)
                elif item[0] == "task" and tasks[item[1]][0] in ("F", "E") and by_pool(tasks[item[1]]):
                    n = item[1]
                    t, g, k = tasks[n], nth(n) % 2, pooled_gates(n)
                    rows = I if t[0] == "E" and t[2] == EP else P
                    dst = (hS if rows == I else ffT[:, t[2], :])[:, t[1] * N:(t[1] + 1) * N]
                    pool.wait_ge(gu_ready, k)
                    half, a = gu[0:rows, g, 0:N], act_u[0:rows, g, :]
                    nc.gpsimd.tensor_tensor(a, act_g[0:rows, g, :], half, ALU.mult).then_inc(pool_chain, 1)
                    pool.wait_ge(pool_chain, 2 * k - 1)
                    nc.gpsimd.tensor_tensor(a, a, half, ALU.add).then_inc(pool_chain, 1)
                    pool.wait_ge(pool_chain, 2 * k)
                    nc.gpsimd.tensor_tensor(dst, a, gu[0:rows, g, N:2 * N], ALU.mult).then_inc(gated_pool, 1)

        @block.tensor
        def _(pe):
            def mm(o, l, r, start=True, stop=True):
                return nc.tensor.matmul(o, l, r, start=start, stop=stop)

            def mm_split(o, w, xt, start=True, stop=True):
                mm(o, w[0], xt[0], start, False)
                mm(o, w[1], xt[0], False, False)
                return mm(o, w[0], xt[1], False, stop)

            def transpose_maxima(o, u):
                pe.wait_ge(c16_ready, u + 1)
                b, hp, o16 = u // HP, u % HP, o.bitcast(F16)
                for it in range(IT):
                    last = nc.tensor.transpose(o16[0:2, it * P:(it + 1) * P], c16[:, b, it, 2 * hp:2 * hp + 2], ident16[:, :])
                return last

            pe.wait_ge(idents, 4)
            for item in order:
                if item[0] == "S":
                    _, u, jp = item
                    n, b, hp = 2 * u + jp, u // HP, u % HP
                    if jp == 0:
                        pe.wait_ge(qb_ready[b % 2][hp], 16 * (b // 2 + 1))
                        pe.wait_ge(crow_ready[b % 2][hp], 16 * (b // 2 + 1))
                        pe.wait_ge(kb_ready, b + 1)
                    if n == 0:
                        pe.wait_ge(consts, 7)
                    if n < 2:
                        for k in range(MB + 2 * n, MB + 2 * n + 2):
                            first = [m for m in range(len(tasks)) if bank_of[m] == k and phase[m] == 0]
                            pe.wait_ge(*read_out(first[-1]))
                    else:
                        pe.wait_ge(ph_ready, n - 1)
                    for j in range(2):
                        k0 = b * J + (2 * jp + j) * P
                        o = psS[:, 2 * (n % 2) + j, :]
                        mm(o, ka[:, k0:k0 + P], qa[:, b % 2, 2 * hp:2 * hp + 2, :], stop=False)
                        last = mm(o, kb[:, k0:k0 + P], qb[:, b % 2, 2 * hp:2 * hp + 2, :], start=False)
                    last.then_inc(s_ready, 1)
                elif item[0] == "PV":
                    _, u, h = item
                    b = u // HP
                    if h == 0:
                        wait_split(pe, 2 * u)
                        wait_split(pe, 2 * u + 1)
                        pe.wait_ge(ph_ready, 2 * u + 2)
                        pe.wait_ge(vl_ready, b + 1)
                        if u >= 1:
                            pe.wait_ge(on_ready, u)
                        else:
                            first = [m for m in range(len(tasks)) if bank_of[m] == MB + 4 and phase[m] == 0]
                            pe.wait_ge(*read_out(first[-1]))
                    for it in range(IT):
                        g = (h * IT + it) * OW
                        o = psO[:, g:g + OW]
                        for jt in range(JT):
                            n = (2 * u + jt // 2) % PSLOTS
                            c0 = (jt % 2) * CH + h * N + it * P
                            v = vm[:, JT * b + jt, :]
                            mm(o, ph[:, n, c0:c0 + P], v[:, 0:OW], start=(jt == 0), stop=False)
                            mm(o[:, 0:DH], ph[:, n, c0:c0 + P], v[:, OW:VW], start=False, stop=False)
                            last = mm(o, pl[:, n, c0:c0 + P], v[:, 0:OW], start=False, stop=(jt == JT - 1))
                    if h == 1:
                        last.then_inc(o_ready, 1)
                elif item[0] == "task":
                    n = item[1]
                    t, k = tasks[n], bank_of[n]
                    o, b, c = banks[k], t[1], t[1]
                    earlier = [m for m in range(n) if bank_of[m] == k]
                    if k < MB or (earlier and phase[earlier[-1]] == phase[n]):
                        if earlier:
                            pe.wait_ge(*read_out(earlier[-1]))
                    elif k < MB + 4 and phase[n] == 2:
                        pe.wait_ge(ph_ready, CHUNKS)
                    elif phase[n] == 2:
                        pe.wait_ge(on_ready, UNITS)
                    if t[0] == "XT":
                        pe.wait_ge(zx_ready[b], 1)
                        for i in range(IT):
                            last = nc.tensor.transpose(o[:, i * P:(i + 1) * P], yx[:, IT * b + i, :], ident[:, :])
                    elif t[0] == "CT":
                        pe.wait_ge(zc_ready[b], 1)
                        for i in range(JT):
                            last = nc.tensor.transpose(o[:, i * P:(i + 1) * P], cs[:, JT * b + i, :], ident[:, :])
                    elif t[0] == "K":
                        if b == 0:
                            pe.wait_ge(ld_k, 48)
                        pe.wait_ge(cnT_ready, b + 1)
                        last = mm(o, wkk[:, :], cnT[:, b % 2 * J:(b % 2 + 1) * J])
                    elif t[0] == "V":
                        pe.wait_ge(cnT_ready, b + 1)
                        for i in range(JT):
                            k0 = b % 2 * J + i * P
                            last = mm(o[:, i * DH:(i + 1) * DH], cnT[:, k0:k0 + P], wv[:, :])
                    elif t[0] == "Q":
                        pe.wait_ge(wl_ready, 1)
                        pe.wait_ge(xnT_ready, b + 1)
                        last = mm_split(o[:, 0:N], [wq[:, i, t[2] * P:(t[2] + 1) * P] for i in range(2)],
                                        [xnT[:, i, b * N:(b + 1) * N] for i in range(2)])
                        if len(t) > 3:
                            last = transpose_maxima(o[:, N:2 * N], t[3])
                    elif t[0] == "M":
                        _, _, h, it = t
                        pe.wait_ge(ka_ready, b + 1)
                        pe.wait_ge(ql_ready, HP * b + h // 2 + 1)
                        last = mm(o, qa[:, b % 2, h, it * P:(it + 1) * P], ka[:, b * J:(b + 1) * J])
                    elif t[0] == "C":
                        last = transpose_maxima(o[:, 0:N], b * HP + t[2])
                    elif t[0] == "F":
                        ft = t[2]
                        pe.wait_ge(wl_ready, 2)
                        pe.wait_ge(xnT_ready, b + 1)
                        for half in range(2):
                            f0 = (1 - half) * FF + ft * P
                            last = mm_split(o[:, half * N:(half + 1) * N], [wf1[:, i, f0:f0 + P] for i in range(2)],
                                            [xnT[:, i, b * N:(b + 1) * N] for i in range(2)])
                    elif t[0] == "T":
                        _, _, it, half = t
                        pe.wait_ge(onl_ready, HP * b + HP // 2 * (half + 1))
                        o16 = o.bitcast(F16)
                        for i in range(8):
                            hp = 4 * half + i % 4
                            last = nc.tensor.transpose(
                                o16[:, i * P:(i + 1) * P],
                                on[:, i // 4, b % 2, it, 2 * hp:2 * hp + 2, :].rearrange("p h d -> p (h d)"), ident16[:, :])
                    elif t[0] in ("W", "WA", "WB"):
                        tt = t[1]
                        hps = {"W": range(HP), "WA": range(HP // 2), "WB": range(HP // 2, HP)}[t[0]]
                        for ft in range(FT):
                            pe.wait_ge(*gated_by("F", tt // IT, ft))
                        pe.wait_ge(ld_m, 64)
                        pe.wait_ge(wl_ready, 4)
                        tc = slice(tt * P, (tt + 1) * P)
                        if t[0] != "WB":
                            for ft in range(FT):
                                mm(o[:, 0:DIM], ffT[:, ft, tc], wf2[:, ft, :], start=(ft == 0), stop=False)
                        pe.wait_ge(oT_ready, 4 * (tt // IT) + {"W": 4, "WA": 2, "WB": 3}[t[0]])
                        if t[0] == "WB" and tt % IT == IT - 1:
                            pe.wait_ge(oT_dve, 1)
                        for hp in hps:
                            last = mm_split(o[:, 0:DIM], [oT[:, i, hp, tt // IT % 2, (tt % IT) * P:(tt % IT + 1) * P]
                                                          for i in range(2)],
                                            [wo[:, i, hp * DIM:(hp + 1) * DIM] for i in range(2)],
                                            start=(t[0] == "WB" and hp == hps[0]), stop=(hp == hps[-1]))
                    elif t[0] == "YT":
                        pe.wait_ge(y2_ready, c + 1)
                        for i in range(IT):
                            last = nc.tensor.transpose(o[:, i * P:(i + 1) * P], yx[:, IT * c + i, :], ident[:, :])
                    elif t[0] == "L":
                        pe.wait_ge(wl_ready, 5)
                        pe.wait_ge(y2T_ready, c + 1)
                        for i in range(IT):
                            t0 = c * N + i * P
                            last = mm_split(o[:, i * E:(i + 1) * E], [y2T[:, k, t0:t0 + P] for k in range(2)],
                                            [wsm[:, k, 2 * I:2 * I + E] for k in range(2)])
                    elif t[0] == "E":
                        p, rows = t[2], P if t[2] < EP else I
                        for half in range(2):
                            ws = [wgu[:, i, half * E * I + p * P:half * E * I + (p + 1) * P] if p < EP
                                  else wsm[:, i, half * I:(half + 1) * I] for i in range(2)]
                            last = mm_split(o[0:rows, half * N:(half + 1) * N], ws,
                                            [y2T[:, i, c * N:(c + 1) * N] for i in range(2)])
                    elif t[0] == "CWT":
                        pe.wait_ge(cw_ready, c + 1)
                        o16 = o.bitcast(F16)
                        for i in range(IT):
                            last = nc.tensor.transpose(o16[0:2 * E, i * P:(i + 1) * P], cw16[:, i, :], ident16[:, :])
                    elif t[0] == "CB":
                        pe.wait_ge(cwT_ready, c + 1)
                        for i in range(2):
                            last = mm(o[:, i * N:(i + 1) * N], esel[:, 2 * t[2] + i, :, :].rearrange("k e i -> k (e i)"),
                                      cwT[:, c % 2, :])
                    elif t[0] == "D":
                        tt = t[1]
                        tc = slice(tt * P, (tt + 1) * P)
                        pe.wait_ge(*gated_by("E", tt // IT, EP))
                        mm(o[:, 0:DIM], hS[:, tc], wds[:, :], stop=False)
                        for p in range(EP):
                            pe.wait_ge(scaled, scaled_by(tt // IT, p))
                            last = mm(o[:, 0:DIM], ffT[:, p, tc], wd[:, p, :], start=False, stop=(p == EP - 1))
                    last.then_inc(ready[k], 1)

        @block.scalar
        def _(act):
            act.dma_start(cs[:, 0:JT, :], c_t[:, 0:JT, :]).then_inc(ld_c[0], 16)
            act.dma_start(lnp[:, 0:1], ln_g.rearrange("(d a) -> d a", a=1)).then_inc(ld_p, 16)
            act.dma_start(lnp[:, 1:2], ln_b.rearrange("(d a) -> d a", a=1)).then_inc(ld_p, 16)
            act.dma_start(lnp[:, 2:3], cln_g.rearrange("(d a) -> d a", a=1)).then_inc(ld_p, 16)
            act.dma_start(lnp[:, 3:4], cln_b.rearrange("(d a) -> d a", a=1)).then_inc(ld_p, 16)
            act.dma_start(gates[:, 0:1], g_xattn.rearrange("(a e) -> a e", a=1).broadcast_to([P, 1])).then_inc(ld_p, 16)
            act.dma_start(gates[:, 1:2], g_ffn.rearrange("(a e) -> a e", a=1).broadcast_to([P, 1])).then_inc(ld_p, 16)

            def sqrt_of(sl):
                return nc.scalar.activation(std[:, sl], vare[:, sl], ACT.Sqrt)

            for item in order:
                if item[0] == "ROOT":
                    b = item[1]
                    act.wait_ge(var_ready[b], 1)
                    sqrt_of(slice(XT + JT * b, XT + JT * (b + 1)))
                    sqrt_of(slice(IT * b, IT * (b + 1))).then_inc(std_ready[b], 1)
                    if b == 0:
                        act.wait_ge(ld_p, 96)
                    if b == B - 1:
                        nc.scalar.activation(tg[:, :], gates[:, :], ACT.Tanh).then_inc(tg_ready, 1)
                elif item[0] == "SPLIT":
                    src, w, loaded, count = splits[item[1]]
                    act.wait_ge(loaded, count)
                    nc.scalar.activation(w[:, 0, :], src, ACT.Copy).then_inc(wh_ready, 1)
                    if item[1] == len(splits) - 1:
                        act.wait_ge(ld_s, 48)
                        nc.scalar.activation(wsm[:, 0, :], wsm32[:, :], ACT.Copy).then_inc(wh_ready, 1)
                elif item[0] == "WARM":
                    sqrt_of(slice(0, 1))
                elif item[0] == "SQ":
                    c = item[1]
                    act.wait_ge(y_var_ready, c + 1)
                    sqrt_of(slice(IT * c, IT * (c + 1))).then_inc(y_std_ready, 1)
                elif item[0] == "S":
                    _, u, jp = item
                    n = 2 * u + jp
                    act.wait_ge(s_ready, n + 1)
                    if n >= 4:
                        wait_split(act, n - 4)
                    else:
                        act.wait_ge(wl_ready, n + 1)
                    if n >= PSLOTS:
                        act.wait_ge(o_ready, u - 2)
                    src = psS[:, 2 * (n % 2):2 * (n % 2) + 2, :]
                    nc.scalar.activation(p32[:, n % 4, :].rearrange("p (j c) -> p j c", j=2), src, ACT.Exp,
                                         scale=SM_SCALE).then_inc(p32_ready, 1)
                    nc.scalar.activation(ph[:, n % PSLOTS, :].rearrange("p (j c) -> p j c", j=2), src, ACT.Exp,
                                         scale=SM_SCALE).then_inc(ph_ready, 1)
                elif item[0] == "task":
                    n = item[1]
                    t = tasks[n]
                    o, b, c = banks[bank_of[n]], t[1], t[1]
                    if t[0] == "CT":
                        act.wait_ge(*stands(n))
                        if b >= 2:
                            act.wait_ge(kb_ready, b - 1)
                            act.wait_ge(vl_ready, b - 1)
                        nc.scalar.activation(cnT[:, b % 2 * J:(b % 2 + 1) * J], o, ACT.Identity, bias=lnp[:, 3:4],
                                             scale=lnp[:, 2:3]).then_inc(cnT_ready, 1)
                    elif t[0] == "K":
                        act.wait_ge(*stands(n))
                        nc.scalar.activation(ka[:, b * J:(b + 1) * J], o, ACT.Copy).then_inc(ka_ready, 1)
                    elif t[0] == "V":
                        act.wait_ge(*stands(n))
                        nc.scalar.activation(vm[:, JT * b:JT * (b + 1), 0:DH],
                                             o[:, 0:JT * DH].rearrange("p (t d) -> p t d", d=DH),
                                             ACT.Copy).then_inc(vh_ready, 1)
                    elif t[0] == "Q":
                        p, s = t[2], b % 2
                        if b >= 2:
                            act.wait_ge(qb_ready[s][p], 16 * (b // 2))
                        act.wait_ge(*stands(n))
                        nc.scalar.activation(qa[0:DH, s, 2 * p, :], o[0:DH, 0:N], ACT.Copy)
                        nc.scalar.activation(qa[0:DH, s, 2 * p + 1, :], o[DH:P, 0:N], ACT.Copy).then_inc(qh_ready, 1)
                    elif t[0] in ("F", "E"):
                        act.wait_ge(*stands(n))
                        g, rows = nth(n), (I if t[0] == "E" and t[2] == EP else P)
                        if g > 2:
                            act.wait_ge(*gate(nth_gate(g - 2)))
                        if t[0] == "E" and b == B - 1:
                            nc.scalar.activation(act_u[0:rows, g % 2, :], o[0:rows, 0:N], ACT.Silu).then_inc(th_ready, 1)
                        else:
                            nc.scalar.activation(act_g[0:rows, g % 2, :], o[0:rows, 0:N], ACT.Tanh, scale=0.5).then_inc(th_ready, 1)
                        if by_pool(t):
                            nc.scalar.activation(gu[0:rows, g % 2, 0:N], o[0:rows, 0:N], ACT.Copy, scale=0.5)
                            nc.scalar.activation(gu[0:rows, g % 2, N:2 * N], o[0:rows, N:2 * N], ACT.Copy).then_inc(gu_ready, 1)
                    elif t[0] == "T" and not by_dve(t):
                        _, _, it, half = t
                        act.wait_ge(*stands(n))
                        if b >= 2:
                            act.wait_ge(x1_ready, IT * (b - 1))
                        nc.scalar.activation(oT[:, :, 4 * half:4 * half + 4, b % 2, it * P:(it + 1) * P],
                                             o.bitcast(F16).rearrange("p (k h c) -> p k h c", k=2, h=4),
                                             ACT.Copy).then_inc(oT_ready, 1)
                    elif t[0] == "L":
                        act.wait_ge(*stands(n))
                        if c >= 1:
                            act.wait_ge(cw_ready, c)
                        nc.scalar.activation(es[:, :, :], o[:, 0:IT * E].rearrange("p (t e) -> p t e", e=E), ACT.Exp,
                                             scale=-1.0).then_inc(es_ready, 1)
                    elif t[0] == "CWT":
                        act.wait_ge(*stands(n))
                        if c >= 2:
                            act.wait_ge(scaled, scaled_by(c - 2, EP - 1))
                        nc.scalar.activation(cwT[:, c % 2, :], o.bitcast(F16)[0:2 * E, 0:N], ACT.Copy).then_inc(cwT_ready, 1)

        @block.vector
        def _(dve):
            done = [0]

            def step(ins):
                done[0] += 1
                ins.then_inc(chain, 1)
                dve.wait_ge(chain, done[0])

            def statistics(tiles):
                for i, src in tiles:
                    last = nc.vector.bn_stats(stats[:, i, :], src)
                step(last)
                for i, _ in tiles:
                    last = nc.vector.bn_aggr(mv[:, i, :], stats[:, i, :])
                step(last)

            def plus_eps(sl):
                return nc.vector.tensor_scalar(vare[:, sl], mv[:, sl, 1], EPS, None, ALU.add)

            def copy_maxima(o, u):
                b, g = u // HP, u % HP
                if b >= 2:
                    dve.wait_ge(crow_ready[b % 2][g], 16 * (b // 2))
                nc.vector.tensor_copy(cT[:, b % 2, g, :], o.bitcast(F16)[0:2, 0:N]).then_inc(cT_ready, 1)

            def inverse(sl):
                return nc.vector.reciprocal(rstd[:, sl], std[:, sl])

            def normalise(dst, src, i):
                return nc.vector.tensor_scalar(dst, src, mv[:, i, 0:1], rstd[:, i:i + 1], ALU.subtract, ALU.mult)

            pair = [P, IT, E, E]

            def route_groups(c):
                gpair = [P, IT, NG, NG]
                dve.wait_ge(es_ready, c + 1)
                step(nc.vector.tensor_scalar(es[:, :, :], es[:, :, :], 1.0, None, ALU.add))
                step(nc.vector.reciprocal(sc[:, :, :], es[:, :, :]))
                step(nc.vector.tensor_tensor(scc[:, :, :], sc[:, :, :],
                                             cb[:, :].unsqueeze(1).broadcast_to([P, IT, E]), ALU.add))
                step(nc.vector.tensor_reduce(grp[:, :, :], scc[:, :, :].rearrange("p t (g m) -> p t g m", m=EPG),
                                             AX_X, ALU.add))
                other, own = grp[:, :, :].unsqueeze(2).broadcast_to(gpair), grp[:, :, :].unsqueeze(3).broadcast_to(gpair)
                a, bb = cmpA[:, :, 0:NG, 0:NG], cmpB[:, :, 0:NG, 0:NG]
                nc.vector.tensor_tensor(a, other, own, ALU.is_gt)
                step(nc.vector.tensor_tensor(bb, other, own, ALU.is_equal))
                step(nc.vector.tensor_tensor(bb, bb, lower[:, 0:NG, 0:NG].unsqueeze(1).broadcast_to(gpair), ALU.mult))
                step(nc.vector.tensor_tensor(a, a, bb, ALU.add))
                step(nc.vector.tensor_reduce(grank[:, :, :], a, AX_X, ALU.add))
                step(nc.vector.tensor_scalar(gsel[:, :, :], grank[:, :, :], float(TKG), None, ALU.is_lt))
                step(nc.vector.tensor_tensor(choice[:, :, :].rearrange("p t (g m) -> p t g m", m=EPG),
                                             scc[:, :, :].rearrange("p t (g m) -> p t g m", m=EPG),
                                             gsel[:, :, :].unsqueeze(3).broadcast_to([P, IT, NG, EPG]), ALU.mult))

            def route_ranks(c):
                other, own = choice[:, :, :].unsqueeze(2).broadcast_to(pair), choice[:, :, :].unsqueeze(3).broadcast_to(pair)
                nc.vector.tensor_tensor(cmpA[:, :, :, :], other, own, ALU.is_gt)
                step(nc.vector.tensor_tensor(cmpB[:, :, :, :], other, own, ALU.is_equal))
                step(nc.vector.tensor_tensor(cmpB[:, :, :, :], cmpB[:, :, :, :],
                                             lower[:, :, :].unsqueeze(1).broadcast_to(pair), ALU.mult))
                step(nc.vector.tensor_tensor(cmpA[:, :, :, :], cmpA[:, :, :, :], cmpB[:, :, :, :], ALU.add))
                step(nc.vector.tensor_reduce(rank[:, :, :], cmpA[:, :, :, :], AX_X, ALU.add))
                step(nc.vector.tensor_scalar(rank[:, :, :], rank[:, :, :], float(TOPK), None, ALU.is_lt))

            def route_weights(c):
                step(nc.vector.tensor_tensor(sc[:, :, :], sc[:, :, :], rank[:, :, :], ALU.mult))
                step(nc.vector.tensor_reduce(wsum[:, :], sc[:, :, :], AX_X, ALU.add))
                step(nc.vector.tensor_scalar(wsum[:, :], wsum[:, :], 1e-20, 1.0 / ROUTE_SCALE, ALU.add, ALU.mult))
                step(nc.vector.reciprocal(wsum[:, :], wsum[:, :]))
                step(nc.vector.tensor_tensor(cw[:, :, :], sc[:, :, :], wsum[:, :].unsqueeze(2).broadcast_to([P, IT, E]),
                                             ALU.mult))
                if c >= 1:
                    dve.wait_ge(cwT_ready, c)
                step(nc.vector.tensor_copy(cw16[:, :, 0:E], cw[:, :, :]))
                nc.vector.tensor_tensor(cw16[:, :, E:2 * E], cw[:, :, :], cw16[:, :, 0:E],
                                        ALU.subtract).then_inc(cw_ready, 1)

            for item in order:
                if item[0] == "STAT":
                    b = item[1]
                    dve.wait_ge(ld_x[b], 16)
                    dve.wait_ge(ld_c[b], 16)
                    xt, ct = range(IT * b, IT * (b + 1)), range(JT * b, JT * (b + 1))
                    statistics([(i, xs[:, i, :]) for i in xt] + [(XT + i, cs[:, i, :]) for i in ct])
                    plus_eps(slice(XT + JT * b, XT + JT * (b + 1)))
                    sl = slice(IT * b, IT * (b + 1))
                    nc.vector.tensor_scalar(vare[:, sl], mv[:, sl, 1], 1.0 + EPS, EPS * EPS, ALU.mult,
                                            ALU.add).then_inc(var_ready[b], 1)
                elif item[0] == "ROOT":
                    b = item[1]
                    dve.wait_ge(std_ready[b], 1)
                    inverse(slice(XT + JT * b, XT + JT * (b + 1)))
                    last = inverse(slice(IT * b, IT * (b + 1)))
                    if b > 0:
                        last.then_inc(rs_ready[b], 1)
                    else:
                        step(last)
                elif item[0] == "NORM" and item[1] == 0:
                    for i in range(IT):
                        last = normalise(yx[:, i, :], xs[:, i, :], i)
                    last.then_inc(zx_ready[0], 1)
                    for i in range(JT):
                        last = normalise(cs[:, i, :], cs[:, i, :], XT + i)
                    last.then_inc(zc_ready[0], 1)
                    dve.wait_ge(ld_p, 96)
                elif item[0] == "NEG":
                    _, b, g = item
                    hs = slice(2 * g, 2 * g + 2)
                    dve.wait_ge(mx_ready, 2 * IT * (HP * b + g + 1))
                    nc.vector.tensor_scalar(c16[:, b, :, hs], mx[:, b, :, hs], -1.0 / SHIFT, None,
                                            ALU.mult).then_inc(c16_ready, 1)
                elif item[0] == "ST":
                    c = item[1]
                    dve.wait_ge(x1_ready, IT * (c + 1))
                    statistics([(i, x1[:, i, :]) for i in range(IT * c, IT * (c + 1))])
                    plus_eps(slice(IT * c, IT * (c + 1))).then_inc(y_var_ready, 1)
                elif item[0] == "SQ":
                    c = item[1]
                    dve.wait_ge(y_std_ready, c + 1)
                    step(inverse(slice(IT * c, IT * (c + 1))))
                    for i in range(IT * c, IT * (c + 1)):
                        last = normalise(yx[:, i, :], x1[:, i, :], i)
                    last.then_inc(y2_ready, 1)
                elif item[0] == "RTA":
                    route_groups(item[1])
                elif item[0] == "RTB":
                    route_ranks(item[1])
                elif item[0] == "RTC":
                    route_weights(item[1])
                elif item[0] == "PL":
                    n = item[1]
                    if n not in pooled:
                        if n >= PSLOTS:
                            dve.wait_ge(o_ready, n // 2 - 2)
                        dve.wait_ge(ph_ready, n + 1)
                        nc.vector.tensor_tensor(pl[:, n % PSLOTS, :], p32[:, n % 4, :], ph[:, n % PSLOTS, :],
                                                ALU.subtract).then_inc(pl_dve, 1)
                elif item[0] == "O":
                    u = item[1]
                    b, hp = u // HP, u % HP
                    dve.wait_ge(o_ready, u + 1)
                    if u >= 2:
                        dve.wait_ge(onl_ready, u - 1)
                    o = psO[:, 0:2 * IT * OW].rearrange("p (h t w) -> p h t w", h=2, w=OW)
                    step(nc.vector.reciprocal(rden[:, u % 2, :, :], o[:, :, :, DH]))
                    nc.vector.tensor_tensor(
                        on32[:, u % 2, :, :, :].rearrange("p t h d -> p h t d"), o[:, :, :, 0:DH],
                        rden[:, u % 2, :, :].unsqueeze(3).broadcast_to([P, 2, IT, DH]), ALU.mult).then_inc(on_ready, 1)
                    dve.wait_ge(on_ready, u + 1)
                    if b >= 2 and hp == 0:
                        dve.wait_ge(oT_ready, 4 * (b - 1))
                    nc.vector.tensor_copy(on[:, 0, b % 2, :, 2 * hp:2 * hp + 2, :], on32[:, u % 2, :, :, :]).then_inc(onh_ready, 1)
                elif item[0] == "task":
                    n = item[1]
                    t = tasks[n]
                    o, b, c = banks[bank_of[n]], t[1], t[1]
                    if t[0] == "XT":
                        dve.wait_ge(*stands(n))
                        cols = slice(b * N, (b + 1) * N)
                        step(nc.vector.tensor_scalar(xn32[:, :], o[:, 0:N], lnp[:, 0:1], lnp[:, 1:2], ALU.mult, ALU.add))
                        step(nc.vector.tensor_copy(xnT[:, 0, cols], xn32[:, :]))
                        nc.vector.tensor_tensor(xnT[:, 1, cols], xn32[:, :], xnT[:, 0, cols],
                                                ALU.subtract).then_inc(xnT_ready, 1)
                    elif t[0] == "K":
                        dve.wait_ge(ka_ready, b + 1)
                        cols = slice(b * J, (b + 1) * J)
                        nc.vector.tensor_tensor(kb[0:DH, cols], o[0:DH, :], ka[0:DH, cols],
                                                ALU.subtract).then_inc(kb_ready, 1)
                    elif t[0] == "V":
                        dve.wait_ge(vh_ready, b + 1)
                        nc.vector.tensor_tensor(vm[:, JT * b:JT * (b + 1), OW:VW],
                                                o[:, 0:JT * DH].rearrange("p (t d) -> p t d", d=DH),
                                                vm[:, JT * b:JT * (b + 1), 0:DH], ALU.subtract).then_inc(vl_ready, 1)
                    elif t[0] == "Q":
                        p, s = t[2], b % 2
                        dve.wait_ge(qh_ready, HP * b + p + 1)
                        if len(t) > 3:
                            copy_maxima(o[:, N:2 * N], t[3])
                        nc.vector.tensor_tensor(qa[DH:P, s, 2 * p, :], o[0:DH, 0:N], qa[0:DH, s, 2 * p, :], ALU.subtract)
                        nc.vector.tensor_tensor(qa[DH:P, s, 2 * p + 1, :], o[DH:P, 0:N], qa[0:DH, s, 2 * p + 1, :],
                                                ALU.subtract).then_inc(ql_ready, 1)
                    elif t[0] == "M":
                        _, _, h, it = t
                        dve.wait_ge(*stands(n))
                        nc.vector.tensor_reduce(mx[:, b, it, h:h + 1], o, AX_X, ALU.max).then_inc(mx_ready, 1)
                    elif t[0] == "C":
                        dve.wait_ge(*stands(n))
                        copy_maxima(o[:, 0:N], b * HP + t[2])
                    elif t[0] == "T" and by_dve(t):
                        _, _, it, half = t
                        dve.wait_ge(*stands(n))
                        nc.vector.tensor_copy(oT[:, :, 4 * half:4 * half + 4, b % 2, it * P:(it + 1) * P],
                                             o.bitcast(F16).rearrange("p (k h c) -> p k h c", k=2, h=4)).then_inc(oT_dve, 1)
                    elif t[0] == "WA":
                        tt = t[1]
                        dve.wait_ge(*stands(n))
                        nc.vector.scalar_tensor_tensor(x1[:, tt, :], o[:, 0:DIM], tg[:, 0:1], xs[:, tt, :],
                                                       ALU.mult, ALU.add).then_inc(xa_ready, 1)
                    elif t[0] in ("W", "WB"):
                        tt = t[1]
                        if t[0] == "WB":
                            dve.wait_ge(xa_ready, tt - IT * (B - 1) + 1)
                        dve.wait_ge(*stands(n))
                        dve.wait_ge(tg_ready, 1)
                        nc.vector.scalar_tensor_tensor(x1[:, tt, :], o[:, 0:DIM], tg[:, 0:1], xs[:, tt, :],
                                                       ALU.mult, ALU.add).then_inc(x1_ready, 1)
                    elif t[0] == "YT":
                        dve.wait_ge(*stands(n))
                        cols = slice(c * N, (c + 1) * N)
                        step(nc.vector.tensor_copy(y2T[:, 0, cols], o[:, 0:N]))
                        nc.vector.tensor_tensor(y2T[:, 1, cols], o[:, 0:N], y2T[:, 0, cols], ALU.subtract).then_inc(y2T_ready, 1)
                    elif t[0] in ("F", "E") and not by_pool(t):
                        g, rows = nth(n), (I if t[0] == "E" and t[2] == EP else P)
                        dst = hS[:, b * N:(b + 1) * N] if rows == I else ffT[:, t[2], b * N:(b + 1) * N]
                        dve.wait_ge(th_ready, g)
                        if t[0] == "E" and b == B - 1:
                            nc.vector.tensor_tensor(dst, o[0:rows, N:2 * N], act_u[0:rows, g % 2, :],
                                                    ALU.mult).then_inc(gated, 1)
                        else:
                            step(nc.vector.scalar_tensor_tensor(act_u[0:rows, g % 2, :], act_g[0:rows, g % 2, :], 1.0,
                                                                o[0:rows, 0:N], ALU.add, ALU.mult))
                            nc.vector.scalar_tensor_tensor(dst, o[0:rows, N:2 * N], 0.5, act_u[0:rows, g % 2, :],
                                                           ALU.mult, ALU.mult).then_inc(gated, 1)
                    elif t[0] == "CB":
                        dve.wait_ge(*stands(n))
                        dve.wait_ge(*gated_by("E", c, 2 * t[2]))
                        dve.wait_ge(*gated_by("E", c, 2 * t[2] + 1))
                        hid = ffT[:, 2 * t[2]:2 * t[2] + 2, c * N:(c + 1) * N]
                        nc.vector.tensor_tensor(hid, hid, o.rearrange("p (e c) -> p e c", e=2), ALU.mult).then_inc(scaled, 1)
                    elif t[0] == "D":
                        dve.wait_ge(*stands(n))
                        nc.vector.scalar_tensor_tensor(outt[:, t[1], :], o[:, 0:DIM], tg[:, 1:2], x1[:, t[1], :],
                                                       ALU.mult, ALU.add).then_inc(out_ready, 1)


_INS = ["x", "ctx_1024", "g_xattn", "g_ffn", "L0_xattn_ln_g", "L0_xattn_ln_b", "L0_xattn_cln_g", "L0_xattn_cln_b",
        "L0_xattn_Wq", "L0_xattn_Wkv", "L0_xattn_Wo", "L0_xattn_Wff1", "L0_xattn_Wff2", "L0_ffn_gate_w",
        "L0_ffn_correction_bias", "L0_ffn_Wg", "L0_ffn_Wu", "L0_ffn_Wd", "L0_ffn_Wg_s", "L0_ffn_Wu_s", "L0_ffn_Wd_s"]


def kernel(**inputs):
    import numpy as _np
    import concourse.bacc as _bacc
    from concourse import mybir as _mybir
    from concourse.bass_utils import run_bass_kernel_spmd as _run

    nc = _bacc.Bacc("TRN2", target_bir_lowering=False, num_devices=1)
    arrays, args = {}, []
    for name in _INS:
        a = _np.asarray(inputs[name])
        if name == "L0_ffn_gate_w":
            a = a.T
        a = _np.ascontiguousarray(a)
        arrays[f"in_{name}"] = a
        args.append(nc.dram_tensor(f"in_{name}", a.shape, _mybir.dt.from_np(a.dtype), kind="ExternalInput").ap())
    shape = _np.asarray(inputs["x"]).shape
    args.append(nc.dram_tensor("out_x", shape, _mybir.dt.float32, kind="ExternalOutput").ap())
    flamingo_gated_moe(nc, *args)
    r = _run(nc, [arrays], core_ids=[0])
    return r.results[0]["out_x"]
```
